# Optimizing a Trainium2 kernel written in Bass

```python
import numpy as np
import jax
import jax.numpy as jnp

def _softmax(x, axis=-1):
    return jax.nn.softmax(x, axis=axis)

def _gelu(x):
    return jax.nn.gelu(x, approximate=True)

def _silu(x):
    return jax.nn.silu(x)

def _sigmoid(x):
    return jax.nn.sigmoid(x)

def _layernorm(x, axis=-1, eps=1e-05):
    m = jnp.mean(x, axis=axis, keepdims=True)
    v = jnp.var(x, axis=axis, keepdims=True)
    return (x - m) / jnp.sqrt(v + eps)

def _scatter_add(tgt, idx, src, axis=0):
    return tgt.at[idx].add(src)

def _segment_sum(src, seg, n):
    return jax.ops.segment_sum(src, seg, n)
kernel_name = 'mk_decoder_postln_d2_seqx_r8_fd39ee'

def setup_inputs(seed: int=0):
    np.random.seed(seed)
    _w = jnp.asarray

    def _rec_inputs():
        import jax
        import jax.numpy as jnp
        _rk = jax.random.key(seed)
        x = 7.22e-05 + 1 * jax.random.normal(jax.random.fold_in(_rk, 1), (4, 256, 256), jnp.float32)
        _lenS = 256 - jax.random.randint(jax.random.fold_in(_rk, 7), (4,), 0, max(1, 256 // 4) + 1, jnp.int32)
        _lenS2 = 1601 - jax.random.randint(jax.random.fold_in(_rk, 8), (4,), 0, max(1, 1601 // 4) + 1, jnp.int32)
        _ctx_512P = jax.random.normal(jax.random.fold_in(_rk, 11), (4, 16, 64), jnp.float32)
        _ctx_512c = jax.random.dirichlet(jax.random.fold_in(_rk, 511), 0.3 * jnp.ones((16,), jnp.float32), (4, 1601))
        _ctx_512t = jnp.einsum('bsk,bkd->bsd', _ctx_512c, _ctx_512P)
        _ctx_512t = _ctx_512t * jax.lax.rsqrt(jnp.mean(jnp.square(_ctx_512t)) + 1e-12) * 0.953939
        ctx_512 = -0.000514642 + 1.00011 * (_ctx_512t + 0.3 * jax.random.normal(jax.random.fold_in(_rk, 611), (4, 1601, 64), jnp.float32))
        return (x, ctx_512)
    x, ctx_512 = _rec_inputs()

    def _L0_attn_setup():
        import jax, jax.numpy as jnp
        import numpy as np
        Q_HEADS, KV_HEADS, HEAD_DIM, WINDOW = (16, 4, 128, 64)
        HIDDEN = 256
        ROPE_BASE = 10000.0

        def _rope_tables(T, head_dim, dtype):
            half = head_dim // 2
            inv_freq = 1.0 / ROPE_BASE ** (jnp.arange(half, dtype=jnp.float32) / half)
            t = jnp.arange(T, dtype=jnp.float32)
            freqs = jnp.outer(t, inv_freq)
            return (jnp.cos(freqs).astype(dtype), jnp.sin(freqs).astype(dtype))

        def _apply_rope(x, cos, sin):
            c = cos[None, :, None, :]
            s = sin[None, :, None, :]
            x1, x2 = jnp.split(x, 2, axis=-1)
            return jnp.concatenate([x1 * c - x2 * s, x1 * s + x2 * c], axis=-1)
        key = jax.random.key(seed)
        ks = jax.random.split(key, 5)
        B, T = (1, 512)
        x = jax.random.normal(ks[0], (B, T, HIDDEN), dtype=jnp.float32)
        sc = 0.02
        wq = jax.random.normal(ks[1], (Q_HEADS * HEAD_DIM, HIDDEN), dtype=jnp.float32) * sc
        wk = jax.random.normal(ks[2], (KV_HEADS * HEAD_DIM, HIDDEN), dtype=jnp.float32) * sc
        wv = jax.random.normal(ks[3], (KV_HEADS * HEAD_DIM, HIDDEN), dtype=jnp.float32) * sc
        wo = jax.random.normal(ks[4], (HIDDEN, Q_HEADS * HEAD_DIM), dtype=jnp.float32) * sc
        return {'x': x, 'wq': wq, 'wk': wk, 'wv': wv, 'wo': wo}
    _L0_attn_all = _L0_attn_setup()
    _L0_attn_in = {k: v for k, v in _L0_attn_all.items() if k in ('wq', 'wk', 'wv', 'wo')}
    del _L0_attn_all

    def _L0_xattn_setup():
        import jax, jax.numpy as jnp
        import numpy as np
        B, S, H, NH, L = (2, 256, 256, 16, 64)
        HD = H // NH
        key = jax.random.key(seed)
        k1, k2, k3, k4, k5 = jax.random.split(key, 5)
        scale = 0.02
        return {'q': jax.random.normal(k1, (B, S, H), dtype=jnp.float32), 'latent_kv': jax.random.normal(k2, (B, S, L), dtype=jnp.float32), 'Wq': jax.random.normal(k3, (H, H), dtype=jnp.float32) * scale, 'Wkv_expand': jax.random.normal(k4, (2 * H, L), dtype=jnp.float32) * scale, 'Wout': jax.random.normal(k5, (H, H), dtype=jnp.float32) * scale}
    _L0_xattn_all = _L0_xattn_setup()
    _L0_xattn_in = {k: v for k, v in _L0_xattn_all.items() if k in ('Wq', 'Wkv_expand', 'Wout')}
    del _L0_xattn_all

    def _L0_ffn_setup():
        import jax, jax.numpy as jnp
        import numpy as np
        E, TOPK, H, I = (8, 2, 256, 512)
        SOFTCAP = 30.0
        key = jax.random.key(seed)
        ks = jax.random.split(key, 5)
        s = 1.0 / np.sqrt(H)
        si = 1.0 / np.sqrt(I)
        return {'hidden_states': jax.random.normal(ks[0], (4, 256, H), jnp.float32), 'w_gate': jax.random.normal(ks[1], (H, E), jnp.float32) * s, 'w1': jax.random.normal(ks[2], (E, H, I), jnp.float32) * s, 'w3': jax.random.normal(ks[3], (E, H, I), jnp.float32) * s, 'w2': jax.random.normal(ks[4], (E, I, H), jnp.float32) * si}
    _L0_ffn_all = _L0_ffn_setup()
    _L0_ffn_in = {k: v for k, v in _L0_ffn_all.items() if k in ('w_gate', 'w1', 'w3', 'w2')}
    del _L0_ffn_all

    def _L1_attn_setup():
        import jax, jax.numpy as jnp
        import numpy as np
        import math
        HQ, HKV = (32, 8)
        key = jax.random.key(seed)
        ks = jax.random.split(key, 5)
        B, S, D = (2, 256, 256)
        hd = D // HQ
        w = lambda k, i, o: jax.random.normal(k, (i, o), jnp.float32) / math.sqrt(i)
        return {'x': jax.random.normal(ks[0], (B, S, D), jnp.float32), 'Wq': w(ks[1], D, D), 'Wk': w(ks[2], D, HKV * hd), 'Wv': w(ks[3], D, HKV * hd), 'Wo': w(ks[4], D, D)}
    _L1_attn_all = _L1_attn_setup()
    _L1_attn_in = {k: v for k, v in _L1_attn_all.items() if k in ('Wq', 'Wk', 'Wv', 'Wo')}
    del _L1_attn_all

    def _L1_xattn_setup():
        import jax, jax.numpy as jnp
        import numpy as np
        B, S, L = (2, 128, 128)
        DIM_Q, H, K, D_C, D_CQ, R = (256, 16, 128, 64, 192, 64)

        def _rope_tables(length, dim):
            inv = 1.0 / 10000.0 ** (jnp.arange(0, dim, 2, dtype=jnp.float32) / dim)
            f = jnp.arange(length, dtype=jnp.float32)[:, None] * inv[None, :]
            sin = jnp.repeat(jnp.sin(f), 2, axis=-1)
            cos = jnp.repeat(jnp.cos(f), 2, axis=-1)
            return (sin, cos)

        def _rotate_half(x):
            half = x.shape[-1] // 2
            return jnp.concatenate([-x[..., half:], x[..., :half]], axis=-1)

        def _apply_rope(x, sin, cos):
            return x * cos + _rotate_half(x) * sin
        key = jax.random.key(seed)
        ks = jax.random.split(key, 8)
        return {'hidden_q': jax.random.normal(ks[0], (B, S, DIM_Q), jnp.float32), 'kv_c': jax.random.normal(ks[1], (B, L, D_C), jnp.float32), 'Wq': jax.random.normal(ks[2], (H * K, DIM_Q), jnp.float32) / np.sqrt(DIM_Q).astype(np.float32), 'w_kc_q': jax.random.normal(ks[3], (H, K, D_CQ), jnp.float32) / np.sqrt(K).astype(np.float32), 'w_kc_kv': jax.random.normal(ks[4], (H, K, D_C), jnp.float32) / np.sqrt(K).astype(np.float32), 'W_qr': jax.random.normal(ks[5], (H, D_CQ, R), jnp.float32) / np.float32(np.sqrt(D_CQ) * np.sqrt(R)), 'W_kr': jax.random.normal(ks[6], (H, D_C, R), jnp.float32) / np.sqrt(D_C).astype(np.float32), 'Wo': jax.random.normal(ks[7], (DIM_Q, H * K), jnp.float32) / np.sqrt(H * K).astype(np.float32)}
    _L1_xattn_all = _L1_xattn_setup()
    _L1_xattn_in = {k: v for k, v in _L1_xattn_all.items() if k in ('Wq', 'w_kc_q', 'w_kc_kv', 'W_qr', 'W_kr', 'Wo')}
    del _L1_xattn_all

    def _L1_ffn_setup():
        import jax, jax.numpy as jnp
        import numpy as np
        B, S, HID = (2, 256, 256)
        NUM_HEADS = 16
        HEAD_DIM = HID // NUM_HEADS
        NUM_EXPERTS = 8
        TOP_K = 2
        INTER = 512
        EPS = 1e-05

        def _rmsnorm(x, w, eps=EPS):
            return x * jax.lax.rsqrt(jnp.mean(x * x, axis=-1, keepdims=True) + eps) * w

        def _moe(x_flat, Wr, Wg, Wu, Wd):
            T = x_flat.shape[0]
            logits = x_flat @ Wr.T
            top_logits, top_idx = jax.lax.top_k(logits, TOP_K)
            probs = jax.nn.softmax(top_logits, axis=-1)
            cw = jnp.zeros((T, NUM_EXPERTS), x_flat.dtype)
            cw = cw.at[jnp.arange(T)[:, None], top_idx].add(probs)
            hg = jnp.einsum('eih,th->eti', Wg, x_flat)
            hu = jnp.einsum('eih,th->eti', Wu, x_flat)
            y = jnp.einsum('ehi,eti->eth', Wd, jax.nn.silu(hg) * hu)
            return jnp.einsum('eth,te->th', y, cw)
        key = jax.random.key(seed)
        ks = jax.random.split(key, 12)
        sd_h = 1.0 / np.sqrt(HID)
        sd_i = 1.0 / np.sqrt(INTER)
        return {'x': jax.random.normal(ks[0], (B, S, HID), jnp.float32), 'Wq': jax.random.normal(ks[1], (HID, HID), jnp.float32) * sd_h, 'Wk': jax.random.normal(ks[2], (HID, HID), jnp.float32) * sd_h, 'Wv': jax.random.normal(ks[3], (HID, HID), jnp.float32) * sd_h, 'Wo': jax.random.normal(ks[4], (HID, HID), jnp.float32) * sd_h, 'w_ln1': jnp.ones((HID,), jnp.float32), 'w_ln2': jnp.ones((HID,), jnp.float32), 'Wr': jax.random.normal(ks[5], (NUM_EXPERTS, HID), jnp.float32) * sd_h, 'Wg': jax.random.normal(ks[6], (NUM_EXPERTS, INTER, HID), jnp.float32) * sd_h, 'Wu': jax.random.normal(ks[7], (NUM_EXPERTS, INTER, HID), jnp.float32) * sd_h, 'Wd': jax.random.normal(ks[8], (NUM_EXPERTS, HID, INTER), jnp.float32) * sd_i}
    _L1_ffn_all = _L1_ffn_setup()
    _L1_ffn_in = {k: v for k, v in _L1_ffn_all.items() if k in ('Wq', 'Wk', 'Wv', 'Wo', 'w_ln1', 'w_ln2', 'Wr', 'Wg', 'Wu', 'Wd')}
    del _L1_ffn_all
    return {'x': x, 'ctx_512': ctx_512, 'L0_attn_wq': _L0_attn_in['wq'], 'L0_attn_wk': _L0_attn_in['wk'], 'L0_attn_wv': _L0_attn_in['wv'], 'L0_attn_wo': _L0_attn_in['wo'], 'L0_xattn_Wq': _L0_xattn_in['Wq'], 'L0_xattn_Wkv_expand': _L0_xattn_in['Wkv_expand'], 'L0_xattn_Wout': _L0_xattn_in['Wout'], 'L0_ffn_w_gate': _L0_ffn_in['w_gate'], 'L0_ffn_w1': _L0_ffn_in['w1'], 'L0_ffn_w3': _L0_ffn_in['w3'], 'L0_ffn_w2': _L0_ffn_in['w2'], 'L1_attn_Wq': _L1_attn_in['Wq'], 'L1_attn_Wk': _L1_attn_in['Wk'], 'L1_attn_Wv': _L1_attn_in['Wv'], 'L1_attn_Wo': _L1_attn_in['Wo'], 'L1_xattn_Wq': _L1_xattn_in['Wq'], 'L1_xattn_w_kc_q': _L1_xattn_in['w_kc_q'], 'L1_xattn_w_kc_kv': _L1_xattn_in['w_kc_kv'], 'L1_xattn_W_qr': _L1_xattn_in['W_qr'], 'L1_xattn_W_kr': _L1_xattn_in['W_kr'], 'L1_xattn_Wo': _L1_xattn_in['Wo'], 'L1_ffn_Wq': _L1_ffn_in['Wq'], 'L1_ffn_Wk': _L1_ffn_in['Wk'], 'L1_ffn_Wv': _L1_ffn_in['Wv'], 'L1_ffn_Wo': _L1_ffn_in['Wo'], 'L1_ffn_w_ln1': _L1_ffn_in['w_ln1'], 'L1_ffn_w_ln2': _L1_ffn_in['w_ln2'], 'L1_ffn_Wr': _L1_ffn_in['Wr'], 'L1_ffn_Wg': _L1_ffn_in['Wg'], 'L1_ffn_Wu': _L1_ffn_in['Wu'], 'L1_ffn_Wd': _L1_ffn_in['Wd']}

def reference(x, ctx_512, L0_attn_wq, L0_attn_wk, L0_attn_wv, L0_attn_wo, L0_xattn_Wq, L0_xattn_Wkv_expand, L0_xattn_Wout, L0_ffn_w_gate, L0_ffn_w1, L0_ffn_w3, L0_ffn_w2, L1_attn_Wq, L1_attn_Wk, L1_attn_Wv, L1_attn_Wo, L1_xattn_Wq, L1_xattn_w_kc_q, L1_xattn_w_kc_kv, L1_xattn_W_qr, L1_xattn_W_kr, L1_xattn_Wo, L1_ffn_Wq, L1_ffn_Wk, L1_ffn_Wv, L1_ffn_Wo, L1_ffn_w_ln1, L1_ffn_w_ln2, L1_ffn_Wr, L1_ffn_Wg, L1_ffn_Wu, L1_ffn_Wd):
    import jax
    import jax.numpy as jnp

    def _L0_attn_ref(x, wq, wk, wv, wo):
        import jax, jax.numpy as jnp
        import numpy as np
        Q_HEADS, KV_HEADS, HEAD_DIM, WINDOW = (16, 4, 128, 64)
        HIDDEN = 256
        ROPE_BASE = 10000.0

        def _rope_tables(T, head_dim, dtype):
            half = head_dim // 2
            inv_freq = 1.0 / ROPE_BASE ** (jnp.arange(half, dtype=jnp.float32) / half)
            t = jnp.arange(T, dtype=jnp.float32)
            freqs = jnp.outer(t, inv_freq)
            return (jnp.cos(freqs).astype(dtype), jnp.sin(freqs).astype(dtype))

        def _apply_rope(x, cos, sin):
            c = cos[None, :, None, :]
            s = sin[None, :, None, :]
            x1, x2 = jnp.split(x, 2, axis=-1)
            return jnp.concatenate([x1 * c - x2 * s, x1 * s + x2 * c], axis=-1)
        B, T, _ = x.shape
        reps = Q_HEADS // KV_HEADS
        scale = 1.0 / np.sqrt(HEAD_DIM)
        q = jnp.einsum('bth,oh->bto', x, wq).reshape(B, T, Q_HEADS, HEAD_DIM)
        k = jnp.einsum('bth,oh->bto', x, wk).reshape(B, T, KV_HEADS, HEAD_DIM)
        v = jnp.einsum('bth,oh->bto', x, wv).reshape(B, T, KV_HEADS, HEAD_DIM)
        cos, sin = _rope_tables(T, HEAD_DIM, x.dtype)
        q = _apply_rope(q, cos, sin)
        k = _apply_rope(k, cos, sin)
        qg = q.reshape(B, T, KV_HEADS, reps, HEAD_DIM)
        scores = jnp.einsum('btgrd,bsgd->bgrts', qg, k) * scale
        idx = jnp.arange(T)
        allowed = (idx[None, :] <= idx[:, None]) & (idx[:, None] - idx[None, :] <= WINDOW)
        scores = jnp.where(allowed[None, None, None], scores, jnp.finfo(scores.dtype).min)
        probs = jax.nn.softmax(scores, axis=-1)
        out = jnp.einsum('bgrts,bsgd->btgrd', probs, v)
        out = out.reshape(B, T, Q_HEADS * HEAD_DIM)
        return jnp.einsum('bto,ho->bth', out, wo)

    def _L0_xattn_ref(q, latent_kv, Wq, Wkv_expand, Wout):
        import jax, jax.numpy as jnp
        import numpy as np
        B, S, H, NH, L = (2, 256, 256, 16, 64)
        HD = H // NH
        b, sq, _ = q.shape
        sk = latent_kv.shape[1]
        qp = q @ Wq.T
        kv = latent_kv @ Wkv_expand.T
        k, v = jnp.split(kv, 2, axis=-1)
        qh = qp.reshape(b, sq, NH, HD).transpose(0, 2, 1, 3)
        kh = k.reshape(b, sk, NH, HD).transpose(0, 2, 1, 3)
        vh = v.reshape(b, sk, NH, HD).transpose(0, 2, 1, 3)
        inv_sqrt_d = 1.0 / jnp.sqrt(jnp.float32(HD))
        scores = jnp.einsum('bhqd,bhkd->bhqk', qh, kh) * inv_sqrt_d
        causal = jnp.tril(jnp.ones((sq, sk), dtype=bool))
        scores = jnp.where(causal, scores, jnp.finfo(scores.dtype).min)
        attn = jax.nn.softmax(scores, axis=-1)
        out = jnp.einsum('bhqk,bhkd->bhqd', attn, vh)
        out = out.transpose(0, 2, 1, 3).reshape(b, sq, H)
        return out @ Wout.T

    def _L0_ffn_ref(hidden_states, w_gate, w1, w3, w2):
        import jax, jax.numpy as jnp
        import numpy as np
        E, TOPK, H, I = (8, 2, 256, 512)
        SOFTCAP = 30.0
        orig_shape = hidden_states.shape
        x = hidden_states.reshape(-1, H)
        logits = x @ w_gate
        logits = SOFTCAP * jnp.tanh(logits / SOFTCAP)
        probs = jax.nn.softmax(logits, axis=-1)
        _, idx = jax.lax.top_k(probs, TOPK)
        mask = jax.nn.one_hot(idx, E, dtype=probs.dtype).sum(-2)
        weights = probs * mask
        out = jnp.zeros_like(x)
        for e in range(E):
            h = jax.nn.silu(x @ w1[e]) * (x @ w3[e])
            out = out + h @ w2[e] * weights[:, e:e + 1]
        return out.reshape(orig_shape)

    def _L1_attn_ref(x, Wq, Wk, Wv, Wo):
        import jax, jax.numpy as jnp
        import numpy as np
        import math
        HQ, HKV = (32, 8)
        B, S, D = x.shape
        hd = D // HQ
        G = HQ // HKV
        scale = 1.0 / math.sqrt(hd)
        q = (x @ Wq).reshape(B, S, HKV, G, hd)
        k = (x @ Wk).reshape(B, S, HKV, hd)
        v = (x @ Wv).reshape(B, S, HKV, hd)
        scores = jnp.einsum('bskgd,btkd->bkgst', q, k) * scale
        causal = jnp.tril(jnp.ones((S, S), dtype=bool))
        scores = jnp.where(causal, scores, jnp.float32(-jnp.inf))
        probs = jax.nn.softmax(scores, axis=-1)
        o = jnp.einsum('bkgst,btkd->bskgd', probs, v)
        o = o.reshape(B, S, D)
        return o @ Wo

    def _L1_xattn_ref(hidden_q, kv_c, Wq, w_kc_q, w_kc_kv, W_qr, W_kr, Wo):
        import jax, jax.numpy as jnp
        import numpy as np
        B, S, L = (2, 128, 128)
        DIM_Q, H, K, D_C, D_CQ, R = (256, 16, 128, 64, 192, 64)

        def _rope_tables(length, dim):
            inv = 1.0 / 10000.0 ** (jnp.arange(0, dim, 2, dtype=jnp.float32) / dim)
            f = jnp.arange(length, dtype=jnp.float32)[:, None] * inv[None, :]
            sin = jnp.repeat(jnp.sin(f), 2, axis=-1)
            cos = jnp.repeat(jnp.cos(f), 2, axis=-1)
            return (sin, cos)

        def _rotate_half(x):
            half = x.shape[-1] // 2
            return jnp.concatenate([-x[..., half:], x[..., :half]], axis=-1)

        def _apply_rope(x, sin, cos):
            return x * cos + _rotate_half(x) * sin
        Bv, Sv, _ = hidden_q.shape
        _, Lv, _ = kv_c.shape
        q_hk = (hidden_q @ Wq.T).reshape(Bv, Sv, H, K)
        q_big = jnp.einsum('bshk,hkq->bshq', q_hk, w_kc_q)
        sin_q, cos_q = _rope_tables(Sv, D_CQ)
        q_big = _apply_rope(q_big, sin_q[None, :, None, :], cos_q[None, :, None, :])
        sin_k, cos_k = _rope_tables(Lv, D_C)
        kv_r = _apply_rope(kv_c, sin_k[None], cos_k[None])
        q_r = jnp.einsum('bshq,hqr->bhsr', q_big, W_qr)
        k_r = jnp.einsum('bld,hdr->bhlr', kv_r, W_kr)
        scores = jnp.einsum('bhsr,bhlr->bhsl', q_r, k_r)
        attn = jax.nn.softmax(scores, axis=-1)
        ctx_c = jnp.einsum('bhsl,bld->bhsd', attn, kv_r)
        ctx_lat = jnp.einsum('bhsd,hkd->bhsk', ctx_c, w_kc_kv)
        ctx = ctx_lat.transpose(0, 2, 1, 3).reshape(Bv, Sv, H * K)
        return ctx @ Wo.T

    def _L1_ffn_ref(x, Wq, Wk, Wv, Wo, w_ln1, w_ln2, Wr, Wg, Wu, Wd):
        import jax, jax.numpy as jnp
        import numpy as np
        B, S, HID = (2, 256, 256)
        NUM_HEADS = 16
        HEAD_DIM = HID // NUM_HEADS
        NUM_EXPERTS = 8
        TOP_K = 2
        INTER = 512
        EPS = 1e-05

        def _rmsnorm(x, w, eps=EPS):
            return x * jax.lax.rsqrt(jnp.mean(x * x, axis=-1, keepdims=True) + eps) * w

        def _moe(x_flat, Wr, Wg, Wu, Wd):
            T = x_flat.shape[0]
            logits = x_flat @ Wr.T
            top_logits, top_idx = jax.lax.top_k(logits, TOP_K)
            probs = jax.nn.softmax(top_logits, axis=-1)
            cw = jnp.zeros((T, NUM_EXPERTS), x_flat.dtype)
            cw = cw.at[jnp.arange(T)[:, None], top_idx].add(probs)
            hg = jnp.einsum('eih,th->eti', Wg, x_flat)
            hu = jnp.einsum('eih,th->eti', Wu, x_flat)
            y = jnp.einsum('ehi,eti->eth', Wd, jax.nn.silu(hg) * hu)
            return jnp.einsum('eth,te->th', y, cw)
        b, s, hid = x.shape
        residual = x
        xn = _rmsnorm(x, w_ln1)
        q = (xn @ Wq.T).reshape(b, s, NUM_HEADS, HEAD_DIM)
        k = (xn @ Wk.T).reshape(b, s, NUM_HEADS, HEAD_DIM)
        v = (xn @ Wv.T).reshape(b, s, NUM_HEADS, HEAD_DIM)
        scale = 1.0 / np.sqrt(HEAD_DIM)
        attn = jnp.einsum('bqhd,bkhd->bhqk', q, k) * scale
        causal = jnp.tril(jnp.ones((s, s), bool))
        attn = jnp.where(causal[None, None], attn, -jnp.inf)
        attn = jax.nn.softmax(attn, axis=-1)
        h = jnp.einsum('bhqk,bkhd->bqhd', attn, v).reshape(b, s, hid)
        x = residual + h @ Wo.T
        residual = x
        xn = _rmsnorm(x, w_ln2)
        moe_out = _moe(xn.reshape(-1, hid), Wr, Wg, Wu, Wd).reshape(b, s, hid)
        return residual + moe_out
    x = _layernorm(x + _L0_attn_ref(x, L0_attn_wq, L0_attn_wk, L0_attn_wv, L0_attn_wo), axis=-1)
    x = _layernorm(x + _L0_xattn_ref(x, ctx_512, L0_xattn_Wq, L0_xattn_Wkv_expand, L0_xattn_Wout), axis=-1)
    x = _layernorm(x + _L0_ffn_ref(x, L0_ffn_w_gate, L0_ffn_w1, L0_ffn_w3, L0_ffn_w2), axis=-1)
    x = _layernorm(x + _L1_attn_ref(x, L1_attn_Wq, L1_attn_Wk, L1_attn_Wv, L1_attn_Wo), axis=-1)
    x = _layernorm(x + _L1_xattn_ref(x, ctx_512, L1_xattn_Wq, L1_xattn_w_kc_q, L1_xattn_w_kc_kv, L1_xattn_W_qr, L1_xattn_W_kr, L1_xattn_Wo), axis=-1)
    x = _layernorm(x + _L1_ffn_ref(x, L1_ffn_Wq, L1_ffn_Wk, L1_ffn_Wv, L1_ffn_Wo, L1_ffn_w_ln1, L1_ffn_w_ln2, L1_ffn_Wr, L1_ffn_Wg, L1_ffn_Wu, L1_ffn_Wd), axis=-1)
    return x

_drawn_inputs = setup_inputs


def setup_inputs(seed=0):
    import zlib

    import numpy as np

    out = dict(_drawn_inputs(seed))
    spreads = {'L1_ffn_w_ln1': (1.0, 0.2), 'L1_ffn_w_ln2': (1.0, 0.2)}
    factors = {'L0_attn_wq': 2.987, 'L0_attn_wk': 2.906, 'L0_xattn_Wq': 26.01}
    for name, (base, spread) in spreads.items():
        noise = np.random.default_rng([zlib.crc32(name.encode()), seed]).standard_normal(out[name].shape)
        drawn = base * np.exp(spread * noise) if base else spread * noise
        out[name] = jnp.asarray(drawn.astype(out[name].dtype))
    for name, factor in factors.items():
        out[name] = (out[name] * factor).astype(out[name].dtype)
    return out
```

```python
from contextlib import ExitStack

import concourse.bass as bass
from concourse import mybir

F32 = mybir.dt.float32
F32R = mybir.dt.float32r
BF16 = mybir.dt.bfloat16
I32 = mybir.dt.int32
U32 = mybir.dt.uint32
ALU = mybir.AluOpType
ACT = mybir.ActivationFunctionType
AX = mybir.AxisListType

P = 128
BATCH, SEQ, D = 4, 256, 256
TILES = BATCH * SEQ // P
DC = D // P
CTX, LAT = 1601, 64
KT = -(-CTX // P)
EPS = 1e-5
MASKED = -1e30


class Queue:

    def __init__(self, engine, sem):
        self.engine, self.sem, self.count, self.passed = engine, sem, 0, {}

    def put(self, instruction):
        instruction.then_inc(self.sem, 1)
        self.count += 1
        return (self.sem, self.count)

    def wait(self, *marks):
        for m in marks:
            if m is None:
                continue
            if isinstance(m, list):
                self.wait(*m)
                continue
            sem, value = m
            if self.passed.get(id(sem), 0) < value:
                self.engine.wait_ge(sem, value)
                self.passed[id(sem)] = value


class Buf:

    def __init__(self, ap):
        self.ap, self.readers, self.ready, self.held = ap, [], None, False

    @property
    def free(self):
        return self.readers

    @free.setter
    def free(self, marks):
        self.readers, self.held = marks, False


class Ring:

    def __init__(self, bufs):
        self.bufs, self.at = bufs, -1

    def next(self):
        self.at += 1
        b = self.bufs[self.at % len(self.bufs)]
        assert not b.held, "its last use has not named its readers yet"
        b.held = True
        return b


def decoder(nc, t, out):
    with ExitStack() as top:
        def sem(name):
            return top.enter_context(nc.semaphore(name))

        pe = Queue(nc.tensor, sem("pe_done"))
        act = Queue(nc.scalar, sem("act_done"))
        dve = Queue(nc.vector, sem("dve_done"))
        pool = Queue(nc.gpsimd, sem("pool_done"))
        sp = Queue(nc.sync, sem("sp_unused"))
        dma_sems = [sem(f"dma_{i}") for i in range(48)]
        dma_uses = [0] * len(dma_sems)
        dma_at = [0]

        def load(queue, dst, src):
            i = dma_at[0] % len(dma_sems)
            dma_at[0] += 1
            dma_uses[i] += 16
            queue.engine.dma_start(dst, src).then_inc(dma_sems[i], 16)
            return (dma_sems[i], dma_uses[i])

        def alloc(scope, name, shape, dtype=F32):
            return scope.enter_context(nc.sbuf_tensor(name, shape, dtype))

        psum = [Buf(top.enter_context(nc.psum_tensor(f"bank{i}", [P, 512], F32))) for i in range(8)]

        def vec(*a, **k):
            return alloc(top, *a, **k)

        ident = vec("ident", [P, P])
        ident_b = vec("ident_b", [P, P], BF16)
        mask_f = vec("mask_f", [P, 448])
        mask_b = vec("mask_b", [P, 448], BF16)
        signs = vec("signs", [P, 8])
        ready_c = [load(sp, ident[:], t["ident"]), load(sp, signs[:], t["signs"]),
                   load(sp, mask_f[:], t["masks"])]
        X = vec("X", [P, TILES, D])
        XT_hi = vec("XT_hi", [P, DC, BATCH * SEQ], F32R)
        XT_lo = vec("XT_lo", [P, DC, BATCH * SEQ], F32R)
        x_loaded = load(act, X[:], t["x"].rearrange("(n p) d -> p n d", p=P))
        dve.wait(ready_c)
        m_masks = [dve.put(nc.vector.tensor_copy(ident_b[:], ident[:])),
                   dve.put(nc.vector.tensor_copy(mask_b[:], mask_f[:]))]
        pe.wait(m_masks)
        window0, window1, causal = mask_b[:, 0:128], mask_b[:, 128:320], mask_b[:, 320:448]

        xt_ready = [None] * BATCH
        xt_read = [[] for _ in range(BATCH)]
        x_ready = [[x_loaded] for _ in range(BATCH)]

        def mm(o, a, b, start, stop):
            return nc.tensor.matmul(o, a, b, start=start, stop=stop, skip_group_check=True)

        def mm3(o, a, b, start, stop):
            mm(o, a[0], b[0], start, False)
            mm(o, a[0], b[1], False, False)
            return mm(o, a[1], b[0], False, stop)

        def tok(b, n=2):
            return slice(b * SEQ, b * SEQ + n * P)

        def split(src, hi, lo, marks, free=(), hi_on=act, lo_on=pool):
            hi_on.wait(*marks, *free)
            if hi_on is act:
                m1 = act.put(nc.scalar.copy(hi, src))
            else:
                m1 = hi_on.put(hi_on.engine.tensor_copy(hi, src))
            lo_on.wait(*marks, *free, m1)
            m2 = lo_on.put(lo_on.engine.tensor_tensor(lo, src, hi.bitcast(F32), ALU.subtract))
            return [m1, m2]

        tiny = Ring([Buf(vec(f"tiny{i}", [P, 64])) for i in range(2)])
        normed = Ring([Buf(vec(f"normed{i}", [P, 2, D])) for i in range(2)])

        def inv_sqrt(v, y, s, marks):
            dve.wait(*marks)
            m = dve.put(nc.vector.tensor_single_scalar(s.bitcast(I32), v.bitcast(I32), 1,
                                                       ALU.logical_shift_right))
            dve.wait(m)
            m = dve.put(nc.vector.tensor_scalar(y.bitcast(I32), s.bitcast(I32), -1.0,
                                                float(0x5F3759DF), ALU.mult, ALU.add))
            for _ in range(3):
                dve.wait(m)
                m = dve.put(nc.vector.scalar_tensor_tensor(s, y, -0.5, y, ALU.mult, ALU.mult))
                dve.wait(m)
                m = dve.put(nc.vector.tensor_tensor(s, s, v, ALU.mult))
                dve.wait(m)
                m = dve.put(nc.vector.scalar_tensor_tensor(y, s, 1.5, y, ALU.add, ALU.mult))
            return m

        def row_stats(b, T, marks):
            ms = []
            dve.wait(*marks, *T.free)
            for i in range(2):
                ms.append(dve.put(nc.vector.bn_stats(T.ap[:, 6 * i:6 * i + 6], X[:, 2 * b + i, :])))
            dve.wait(*ms)
            for i in range(2):
                m = dve.put(nc.vector.bn_aggr(T.ap[:, 12 + 2 * i:14 + 2 * i], T.ap[:, 6 * i:6 * i + 6]))
            return m

        def layer_norm(b, marks):
            T = tiny.next()
            m = row_stats(b, T, marks)
            st = T.ap[:, 12:16].rearrange("p (t s) -> p t s", s=2)
            v, y, s = T.ap[:, 16:18], T.ap[:, 18:20], T.ap[:, 20:22]
            dve.wait(m)
            m = dve.put(nc.vector.tensor_scalar(v, st[:, :, 1], EPS, None, ALU.add))
            m = inv_sqrt(v, y, s, [m])
            dve.wait(m)
            ms = []
            for i in range(2):
                ms.append(dve.put(nc.vector.tensor_scalar(
                    X[:, 2 * b + i, :], X[:, 2 * b + i, :], T.ap[:, 12 + 2 * i:13 + 2 * i],
                    T.ap[:, 18 + i:19 + i], ALU.subtract, ALU.mult)))
            T.free = ms
            x_ready[b] = ms
            return ms

        def to_xt(b, src, marks, bank, weight=None):
            pe.wait(*marks, *bank.free, *ready_c)
            view = bank.ap[:, :].rearrange("p (c t) -> p c t", c=DC)
            for i in range(2):
                for c in range(DC):
                    last = nc.tensor.transpose(view[:, c, i * P:(i + 1) * P],
                                               src[:, i, c * P:(c + 1) * P], ident[:])
            m = pe.put(last)
            hi, lo = XT_hi[:, :, tok(b)], XT_lo[:, :, tok(b)]
            act.wait(m, *xt_read[b])
            dve.wait(m, *xt_read[b])
            if weight is None:
                m1 = act.put(nc.scalar.copy(hi, view))
                dve.wait(m1)
                m2 = dve.put(nc.vector.tensor_tensor(lo, view, hi.bitcast(F32), ALU.subtract))
                ms = [m1, m2]
            else:
                w = [weight[:, c:c + 1] for c in range(DC)]
                ms = [act.put(nc.scalar.activation(hi[:, c, :], view[:, c, :], ACT.Copy, scale=w[c]))
                      for c in range(DC)]
                dve.wait(*ms)
                ms += [dve.put(nc.vector.scalar_tensor_tensor(
                    lo[:, c, :], view[:, c, :], w[c], hi[:, c, :].bitcast(F32), ALU.mult, ALU.subtract))
                    for c in range(DC)]
            bank.free = ms
            xt_ready[b] = ms
            xt_read[b] = []
            return m

        def advance(g, n=1):
            for _ in range(n):
                if g is not None:
                    next(g, None)

        def settle():
            marks = [(q.sem, q.count) for q in (pe, act, dve, pool)]
            for q in (sp, pe, act, dve, pool):
                q.wait(*marks)

        stores = []

        def layer0_attention():
            H, G, HD = 16, 4, 128
            REP = H // G
            scale = float(HD) ** -0.5
            with ExitStack() as sc:
                def A(*a, **k):
                    return alloc(sc, *a, **k)
                stage = Ring([Buf(A(f"a_stage{i}", [P, 2048])) for i in range(3)])
                xT = A("a_xT", [P, DC, BATCH * SEQ])
                wkv = [A(f"a_wkv_{s}", [P, DC, 2 * G * HD], F32R) for s in ("hi", "lo")]
                wq = [A(f"a_wq_{s}", [P, G, DC, REP * HD], F32R) for s in ("hi", "lo")]
                wo = [A(f"a_wo_{s}", [P, H, D], F32R) for s in ("hi", "lo")]
                rope = A("a_rope", [P, 2, SEQ])
                kT = [Ring([Buf(A(f"a_kT{i}_{s}", [P, G, SEQ], F32R)) for i in range(2)]) for s in ("hi", "lo")]
                V = Ring([Buf(A(f"a_V{i}", [P, 2, G * HD])) for i in range(2)])
                qT = Ring([Buf([A(f"a_qT{i}_{s}", [P, 2, SEQ], F32R) for s in ("hi", "lo")]) for i in range(4)])
                t1 = Ring([Buf(A(f"a_t1_{i}", [P, 2, SEQ])) for i in range(2)])
                t2 = Ring([Buf(A(f"a_t2_{i}", [P, 2, SEQ])) for i in range(2)])
                Pm = Ring([Buf(A(f"a_P{i}", [P, 384])) for i in range(3)])
                PT = Ring([Buf(A(f"a_PT{i}", [P, 384])) for i in range(2)])
                OT = Ring([Buf([A(f"a_OT{i}_{s}", [P, SEQ], F32R) for s in ("hi", "lo")]) for i in range(2)])
                st = Ring([Buf(A(f"a_st{i}", [P, 8])) for i in range(4)])

                m_xT = load(sp, xT[:], t["xT"].rearrange("(c p) n -> p c n", p=P))
                m_rope = load(act, rope[:], t["rope0"])
                kv_stage = stage.next()
                m = load(sp, kv_stage.ap[:], t["a_wkv"])
                for b in range(BATCH):
                    xt_ready[b] = split(xT[:, :, tok(b)], XT_hi[:, :, tok(b)], XT_lo[:, :, tok(b)],
                                        [m_xT], lo_on=dve)
                    if b == 0:
                        kv_ready = split(kv_stage.ap[:].rearrange("p (c n) -> p c n", c=DC),
                                         wkv[0][:], wkv[1][:], [m], lo_on=dve)
                        kv_stage.free = kv_ready
                wq_ready = []
                for h2 in range(2):
                    s = stage.next()
                    sp.wait(*s.free)
                    m = load(sp, s.ap[:], t["a_wq"][h2])
                    v = s.ap[:].rearrange("p (g c n) -> p g c n", g=2, c=DC)
                    for g in range(2):
                        r = split(v[:, g], wq[0][:, 2 * h2 + g], wq[1][:, 2 * h2 + g], [m], lo_on=pool)
                        wq_ready.append(r)
                    s.free = wq_ready[-1] + wq_ready[-2]
                wo_ready = []

                def load_wo(h2):
                    s = stage.next()
                    sp.wait(*s.free)
                    m = load(sp, s.ap[:], t["a_wo"][h2])
                    v = s.ap[:].rearrange("p (h n) -> p h n", n=D)
                    s.free = split(v, wo[0][:, 8 * h2:8 * h2 + 8], wo[1][:, 8 * h2:8 * h2 + 8], [m])
                    wo_ready.append(s.free)

                for p_ in Pm.bufs:
                    p_.free = [pool.put(nc.gpsimd.memset(p_.ap[:, 128:192], 0.0))]

                proj = Ring(psum[0:2])
                score = Ring(psum[2:4])
                pt_bank = Ring(psum[4:5])
                o_bank = Ring(psum[5:6])
                acc_bank = Ring(psum[6:7])
                misc = psum[7]

                def rotate(bank, m, hi, lo, free):
                    src = bank.ap[:, :].rearrange("p (h n) -> p h n", h=2)
                    a, b_ = t1.next(), t2.next()
                    dve.wait(m, m_rope, *a.free, *b_.free)
                    cos = rope[:, 0:1, :].broadcast_to([P, 2, SEQ])
                    ms = [dve.put(nc.vector.tensor_tensor(a.ap[:], src, cos, ALU.mult))]
                    for o, i in ((0, 64), (64, 0)):
                        sin = rope[i:i + 64, 1:2, :].broadcast_to([64, 2, SEQ])
                        ms.append(dve.put(nc.vector.tensor_tensor(b_.ap[o:o + 64], src[i:i + 64], sin, ALU.mult)))
                    bank.free = ms
                    pool.wait(*ms)
                    m = pool.put(nc.gpsimd.tensor_tensor(a.ap[:], a.ap[:], b_.ap[:], ALU.add))
                    b_.free = [m]
                    r = split(a.ap[:], hi, lo, [m], free)
                    a.free = r
                    return r

                class Batch:
                    pass

                bt = {}

                def kv_project(b):
                    s = bt[b] = Batch()
                    s.k = [r.next() for r in kT]
                    s.v = V.next()
                    s.k_ready = []
                    for gp in range(G // 2):
                        bank = proj.next()
                        pe.wait(*kv_ready, *xt_ready[b], *bank.free)
                        for j in range(2):
                            g = 2 * gp + j
                            for c in range(DC):
                                w = [x[:, c, g * HD:(g + 1) * HD] for x in wkv]
                                last = mm3(bank.ap[:, j * SEQ:(j + 1) * SEQ], w,
                                           (XT_hi[:, c, tok(b)], XT_lo[:, c, tok(b)]), c == 0, c == DC - 1)
                        m = pe.put(last)
                        s.k_ready += rotate(bank, m, s.k[0].ap[:, 2 * gp:2 * gp + 2, :],
                                            s.k[1].ap[:, 2 * gp:2 * gp + 2, :], s.k[0].free)
                        yield
                    ms = []
                    for i in range(2):
                        bank = proj.next()
                        pe.wait(*bank.free)
                        cols = slice(b * SEQ + i * P, b * SEQ + (i + 1) * P)
                        for c in range(DC):
                            last = mm3(bank.ap[:, :], (XT_hi[:, c, cols], XT_lo[:, c, cols]),
                                       [x[:, c, G * HD:] for x in wkv], c == 0, c == DC - 1)
                        m = pe.put(last)
                        act.wait(m, *s.v.free)
                        m = act.put(nc.scalar.copy(s.v.ap[:, i, :], bank.ap[:, :]))
                        bank.free = [m]
                        ms.append(m)
                        yield
                    s.v_ready = ms

                def q_project(b, hp):
                    g, j0 = hp // 2, (hp % 2) * 2
                    bank = proj.next()
                    q = qT.next()
                    pe.wait(*wq_ready[g], *xt_ready[b], *bank.free)
                    for j in range(2):
                        for c in range(DC):
                            w = [x[:, g, c, (j0 + j) * HD:(j0 + j + 1) * HD] for x in wq]
                            last = mm3(bank.ap[:, j * SEQ:(j + 1) * SEQ], w,
                                       (XT_hi[:, c, tok(b)], XT_lo[:, c, tok(b)]), c == 0, c == DC - 1)
                    m = pe.put(last)
                    if hp == H // 2 - 1:
                        xt_read[b].append(m)
                    q.ready = rotate(bank, m, q.ap[0][:], q.ap[1][:], q.free)
                    return q

                def scores(b, h, q):
                    s = bt[b]
                    g, j = h // REP, h % 2
                    bank = score.next()
                    pe.wait(*s.k_ready, *q.ready, *bank.free)
                    kh, kl = s.k[0].ap[:, g, :], s.k[1].ap[:, g, :]
                    for i in range(2):
                        o = bank.ap[:, i * SEQ:(i + 1) * SEQ]
                        rows = slice(i * P, (i + 1) * P)
                        mm3(o, (q.ap[0][:, j, rows], q.ap[1][:, j, rows]), (kh, kl), True, False)
                        if i == 0:
                            last = mm(bank.ap[:, 0:128], ident_b[:], window0, False, True)
                        else:
                            last = mm(bank.ap[:, 320:512], ident_b[:], window1, False, True)
                    m = pe.put(last)
                    if j == 1:
                        q.free = [m]
                    S = st.next()
                    p_ = Pm.next()
                    dve.wait(m, *S.free)
                    views = (bank.ap[:, 0:128], bank.ap[:, 320:512])
                    outs = (p_.ap[:, 0:128], p_.ap[:, 192:384])
                    ms = [dve.put(nc.vector.tensor_reduce(S.ap[:, i:i + 1], views[i], AX.X, ALU.max, negate=True))
                          for i in range(2)]
                    dve.wait(*ms)
                    m = dve.put(nc.vector.tensor_scalar(S.ap[:, 2:4], S.ap[:, 0:2], scale, None, ALU.mult))
                    act.wait(m, *p_.free)
                    ms = [act.put(nc.scalar.activation(outs[i], views[i], ACT.Exp, bias=S.ap[:, 2 + i:3 + i],
                                                       scale=scale, accum_out=S.ap[:, 4 + i:5 + i]))
                          for i in range(2)]
                    bank.free = ms
                    dve.wait(*ms)
                    m = dve.put(nc.vector.reciprocal(S.ap[:, 6:8], S.ap[:, 4:6]))
                    dve.wait(m)
                    p_.ready = [dve.put(nc.vector.tensor_scalar(outs[i], outs[i], S.ap[:, 6 + i:7 + i], None,
                                                                ALU.mult)) for i in range(2)]
                    S.free = p_.ready
                    return p_

                def turn(b, h, p_):
                    bank = pt_bank.next()
                    pe.wait(*p_.ready, *bank.free)
                    for i in range(3):
                        last = nc.tensor.transpose(bank.ap[:, i * P:(i + 1) * P], p_.ap[:, i * P:(i + 1) * P], ident[:])
                    m = pe.put(last)
                    p_.free = [m]
                    x = PT.next()
                    act.wait(m, *x.free)
                    m = act.put(nc.scalar.copy(x.ap[:], bank.ap[:, 0:384]))
                    bank.free = [m]
                    x.ready = [m]
                    return x

                def values(b, h, x):
                    s, g = bt[b], h // REP
                    bank = o_bank.next()
                    pe.wait(*x.ready, *s.v_ready, *bank.free)
                    mm(bank.ap[:, 0:256], s.v.ap[:, 0, g * HD:(g + 1) * HD], x.ap[:, 0:256], True, False)
                    m = pe.put(mm(bank.ap[:, 128:256], s.v.ap[:, 1, g * HD:(g + 1) * HD], x.ap[:, 256:384], False, True))
                    x.free = [m]
                    if h == H - 1:
                        s.v.free = [m]
                        s.k[0].free = s.k[1].free = [m]
                    o = OT.next()
                    o.ready = split(bank.ap[:, 0:256], o.ap[0][:], o.ap[1][:], [m], o.free, lo_on=dve)
                    bank.free = o.ready
                    return o

                def project_out(b, h, o):
                    s = bt[b]
                    if h == 0:
                        s.acc = acc_bank.next()
                        pe.wait(*s.acc.free)
                    pe.wait(*o.ready, *wo_ready[h // 8])
                    for i in range(2):
                        rows = slice(i * P, (i + 1) * P)
                        last = mm3(s.acc.ap[:, i * D:(i + 1) * D], (o.ap[0][:, rows], o.ap[1][:, rows]),
                                   [w[:, h, :] for w in wo], h == 0 and i == 0, h == H - 1)
                    o.free = [pe.put(last)]

                def finish(b):
                    s = bt[b]
                    dve.wait(*pe_mark(), *x_ready[b])
                    v = s.acc.ap[:, :].rearrange("p (t n) -> p t n", t=2)
                    m = dve.put(nc.vector.tensor_tensor(X[:, 2 * b:2 * b + 2, :], v, X[:, 2 * b:2 * b + 2, :], ALU.add))
                    s.acc.free = [m]
                    ms = layer_norm(b, [m])
                    yield
                    yield
                    to_xt(b, X[:, 2 * b:2 * b + 2, :], ms, misc)
                    yield

                def pe_mark():
                    return [(pe.sem, pe.count)]

                N = BATCH * H
                qs, ps, xs, os_ = {}, {}, {}, {}
                for _ in kv_project(0):
                    pass
                qs[0] = q_project(0, 0)
                load_wo(0)
                load_wo(1)
                side = None
                tail = None
                for i in range(N + 4):
                    b, h = divmod(i, H)
                    if i < N:
                        if i % 2 == 0 and i + 2 < N:
                            b2, h2 = divmod(i + 2, H)
                            if h2 == 0 and side is not None:
                                for _ in side:
                                    pass
                            qs[i // 2 + 1] = q_project(b2, h2 // 2)
                        ps[i] = scores(b, h, qs[i // 2])
                    if h == 6 and b + 1 < BATCH:
                        side = kv_project(b + 1)
                    if h >= 6:
                        advance(side)
                    if 0 <= i - 2 < N:
                        xs[i - 2] = turn(*divmod(i - 2, H), ps[i - 2])
                    if 0 <= i - 3 < N:
                        os_[i - 3] = values(*divmod(i - 3, H), xs[i - 3])
                    advance(tail)
                    if 0 <= i - 4 < N:
                        project_out(*divmod(i - 4, H), os_[i - 4])
                        if (i - 4) % H == H - 1:
                            tail = finish((i - 4) // H)
                            advance(tail)
                for _ in tail:
                    pass
                return pe_mark()

        def narrow_attention(name, hd, heads, kv_heads, weights, k_contraction, q_sign, k_sign,
                             expand, source, out_of):
            scale = float(hd) ** -0.5
            T = P // (4 * hd)
            U = heads // T
            PAIRS = T // 2
            per_out = P // hd
            rep = heads // kv_heads
            gap = P - hd
            kc = t[weights[1]].shape[1]
            kvw = kv_heads * hd
            with ExitStack() as sc:
                def A(n, *a, **k):
                    return alloc(sc, f"{name}_{n}", *a, **k)

                def weight(n, key, chunks, width, on):
                    s = A(n + "_stage", [P, chunks, width])
                    w = [A(f"{n}_{x}", [P, chunks, width], F32R) for x in ("hi", "lo")]
                    m = load(sp, s[:], t[key])
                    return w, split(s[:], w[0][:], w[1][:], [m], hi_on=on)

                wq, wq_ready = weight("wq", weights[0], DC, heads * 4 * hd, act)
                wk, wk_ready = weight("wk", weights[1], kc, heads * 4 * hd, act)
                wv, wv_ready = weight("wv", weights[2], kc, kvw, act)
                wo, wo_ready = weight("wo", weights[3], DC, D, act)
                ex = A("expand", [heads, 2, P])
                ex_ready = load(sp, ex[:], t[expand])

                V = Ring([Buf(A(f"V{i}", [P, 2, kv_heads, P + gap])) for i in range(2)])
                for v in V.bufs:
                    v.free = [pool.put(nc.gpsimd.memset(v.ap[:], 0.0))]
                kbd = Ring([Buf(A(f"kbd{i}", [P, T, SEQ], F32R)) for i in range(2)])
                for v in kbd.bufs:
                    v.free = [dve.put(nc.vector.memset(v.ap[:].bitcast(F32), 0.0))]
                qpack = Ring([Buf(A(f"qpack{i}", [P, SEQ], F32R)) for i in range(2)])
                parts = Ring([Buf(A(f"parts{i}", [P, 512], F32R)) for i in range(2)])
                P0 = Ring([Buf(A(f"P0_{i}", [P, T, P])) for i in range(2)])
                P1 = Ring([Buf(A(f"P1_{i}", [P, T, SEQ])) for i in range(2)])
                PT = Ring([Buf(A(f"PT{i}", [P, 384])) for i in range(3)])
                st = Ring([Buf(A(f"st{i}", [P, 4 * T])) for i in range(3)])
                sums = Ring([Buf(A(f"sums{i}", [P, 2, heads])) for i in range(2)])
                rT = Ring([Buf(A(f"rT{i}", [heads, SEQ])) for i in range(2)])
                R = Ring([Buf(A(f"R{i}", [P, SEQ])) for i in range(2)])
                OT = Ring([Buf([A(f"OT{i}_{x}", [P, 2, SEQ], F32R) for x in ("hi", "lo")]) for i in range(2)])

                heads_out = Ring([Buf(A(f"heads_out{i}", [P, 1, SEQ])) for i in range(4)])
                proj = Ring(psum[0:1])
                S0 = Ring(psum[1:2])
                S1 = Ring(psum[2:4])
                pt_bank = Ring(psum[4:6])
                o_bank = Ring(psum[6:7])
                misc = psum[7]

                class Batch:
                    pass

                bt = {}

                def value_project(b):
                    s = bt[b] = Batch()
                    s.v, s.sums, s.rT, s.OT = V.next(), sums.next(), rT.next(), OT.next()
                    s.v_ready, s.O_ready = [], []
                    marks, parts_of = k_contraction(b)
                    for i in range(2):
                        pe.wait(*wv_ready, *marks, *misc.free)
                        n = 0
                        prods = [(l, r) for c in range(kc) for l, r in parts_of(c, i, [w[:, c, :] for w in wv])]
                        for n, (l, r) in enumerate(prods):
                            last = mm(misc.ap[:, 0:kvw], l, r, n == 0, n == len(prods) - 1)
                        m = pe.put(last)
                        act.wait(m, *s.v.free)
                        m = act.put(nc.scalar.copy(s.v.ap[:, i, :, gap:gap + hd],
                                                   misc.ap[:, 0:kvw].rearrange("p (h d) -> p h d", d=hd)))
                        misc.free = [m]
                        s.v_ready.append(m)
                        yield

                def qk_project(b, u):
                    bank, h_, q, k = proj.next(), parts.next(), qpack.next(), kbd.next()
                    cols = slice(u * P, (u + 1) * P)
                    src_hi, src_lo = source
                    pe.wait(*wq_ready, *xt_ready[b], *bank.free)
                    for c in range(DC):
                        mm3(bank.ap[:, 0:SEQ], [w[:, c, cols] for w in wq],
                            (src_hi[:, c, tok(b)], src_lo[:, c, tok(b)]), c == 0, c == DC - 1)
                    marks, parts_of = k_contraction(b)
                    pe.wait(*wk_ready, *marks)
                    prods = [(l, r) for c in range(kc) for r, l in parts_of(c, None, [w[:, c, cols] for w in wk])]
                    for n, (l, r) in enumerate(prods):
                        last = mm(bank.ap[:, SEQ:], l, r, n == 0, n == len(prods) - 1)
                    m = pe.put(last)
                    if u == U - 1:
                        xt_read[b].append(m)
                    act.wait(m, *h_.free)
                    m1 = act.put(nc.scalar.copy(h_.ap[:], bank.ap[:, :]))
                    dve.wait(m1, *q.free, *k.free)
                    hv = h_.ap[:].bitcast(F32)
                    q.ready = [dve.put(nc.vector.scalar_tensor_tensor(
                        q.ap[:], hv[:, 0:SEQ], signs[:, q_sign:q_sign + 1], bank.ap[:, 0:SEQ], ALU.mult, ALU.add))]
                    k.ready = []
                    R_ = P // T
                    for j in range(T):
                        rows = slice(j * R_, (j + 1) * R_)
                        k.ready.append(dve.put(nc.vector.scalar_tensor_tensor(
                            k.ap[rows, j, :], hv[rows, SEQ:], signs[rows, k_sign:k_sign + 1],
                            bank.ap[rows, SEQ:], ALU.mult, ALU.add)))
                    h_.free = bank.free = q.ready + k.ready
                    return q, k

                def scores(b, u, qk):
                    q, k = qk
                    s = bt[b]
                    p0, p1, S = P0.next(), P1.next(), st.next()
                    p0.ready, p1.ready = [], []
                    bank0 = S0.next()
                    pe.wait(*q.ready, *k.ready, *bank0.free)
                    w0 = T * P
                    v0 = bank0.ap[:, 0:w0].rearrange("p (h n) -> p h n", h=T)
                    mm(v0, q.ap[:, 0:P], k.ap[:, :, 0:P], True, False)
                    for j in range(T):
                        last = mm(v0[:, j, :], ident_b[:], causal, False, j == T - 1)
                    m = pe.put(last)
                    dve.wait(m, *S.free)
                    m0 = dve.put(nc.vector.tensor_reduce(S.ap[:, 0:T], v0, AX.X, ALU.max, negate=True))
                    views = []
                    ms = []
                    for pr in range(PAIRS):
                        bank = S1.next()
                        pe.wait(*bank.free)
                        v = bank.ap[:, :].rearrange("p (h n) -> p h n", h=2)
                        mm(bank.ap[:, :], q.ap[:, P:SEQ], k.ap[:, 2 * pr:2 * pr + 2, :], True, False)
                        for j in range(2):
                            last = mm(v[:, j, P:SEQ], ident_b[:], causal, False, j == 1)
                        m = pe.put(last)
                        dve.wait(m)
                        ms.append(dve.put(nc.vector.tensor_reduce(S.ap[:, T + 2 * pr:T + 2 * pr + 2], v, AX.X,
                                                                  ALU.max, negate=True)))
                        views.append((bank, v))
                    q.free = k.free = [m]
                    dve.wait(m0, *ms)
                    m = dve.put(nc.vector.tensor_scalar(S.ap[:, 2 * T:4 * T], S.ap[:, 0:2 * T], scale, None, ALU.mult))
                    act.wait(m, *p0.free, *p1.free, *s.sums.free)
                    for j in range(T):
                        p0.ready.append(act.put(nc.scalar.activation(
                            p0.ap[:, j, :], v0[:, j, :], ACT.Exp, bias=S.ap[:, 2 * T + j:2 * T + j + 1],
                            scale=scale, accum_out=s.sums.ap[:, 0, u * T + j:u * T + j + 1])))
                    bank0.free = list(p0.ready)
                    for j in range(T):
                        bank, v = views[j // 2]
                        p1.ready.append(act.put(nc.scalar.activation(
                            p1.ap[:, j, :], v[:, j % 2, :], ACT.Exp, bias=S.ap[:, 3 * T + j:3 * T + j + 1],
                            scale=scale, accum_out=s.sums.ap[:, 1, u * T + j:u * T + j + 1])))
                        bank.free = [p1.ready[-1]]
                    S.free = [p1.ready[-1]]
                    s.sums_ready = [p0.ready[-1], p1.ready[-1]]
                    return p0, p1

                def turn(u, j, ps):
                    p0, p1 = ps
                    bank, x = pt_bank.next(), PT.next()
                    pe.wait(p0.ready[j], p1.ready[j], *bank.free)
                    for n, src in enumerate((p0.ap[:, j, :], p1.ap[:, j, 0:P], p1.ap[:, j, P:SEQ])):
                        last = nc.tensor.transpose(bank.ap[:, n * P:(n + 1) * P], src, ident[:])
                    m = pe.put(last)
                    if j == T - 1:
                        p0.free = p1.free = [m]
                    eng = act if (u * T + j) % 2 == 0 else dve
                    eng.wait(m, *x.free)
                    if eng is act:
                        m = act.put(nc.scalar.copy(x.ap[:], bank.ap[:, 0:384]))
                    else:
                        m = dve.put(nc.vector.tensor_copy(x.ap[:], bank.ap[:, 0:384]))
                    bank.free = x.ready = [m]
                    return x

                def values(b, h, x):
                    s = bt[b]
                    at = h % per_out
                    if at == 0:
                        s.o = o_bank.next()
                        pe.wait(*s.o.free)
                    lo_ = gap - at * hd
                    w = [s.v.ap[:, i, h // rep, lo_:lo_ + P] for i in range(2)]
                    pe.wait(*x.ready, *s.v_ready)
                    mm(s.o.ap[:, 0:SEQ], w[0], x.ap[:, 0:SEQ], at == 0, False)
                    m = pe.put(mm(s.o.ap[:, P:SEQ], w[1], x.ap[:, SEQ:384], False, at == per_out - 1))
                    x.free = [m]
                    if h == heads - 1:
                        s.v.free = [m]
                    if at == per_out - 1:
                        g = h // per_out
                        o32 = heads_out.next()
                        s.o32 = [o32] if g == 0 else s.o32 + [o32]
                        dve.wait(m, *o32.free)
                        r = dve.put(nc.vector.tensor_copy(o32.ap[:, 0, :], s.o.ap[:, 0:SEQ]))
                        s.o.free = [r]
                        s.O_ready.append(r)

                def finish(b):
                    s = bt[b]
                    dve.wait(*s.sums_ready)
                    m = dve.put(nc.vector.reciprocal(s.sums.ap[:], s.sums.ap[:]))
                    pe.wait(m, *misc.free)
                    for i in range(2):
                        last = nc.tensor.transpose(misc.ap[0:heads, i * P:(i + 1) * P], s.sums.ap[:, i, :], ident[:])
                    m = pe.put(last)
                    s.sums.free = [m]
                    yield
                    act.wait(m, *s.rT.free)
                    m = act.put(nc.scalar.copy(s.rT.ap[:], misc.ap[0:heads, 0:SEQ]))
                    misc.free = [m]
                    ready = []
                    for g in range(2):
                        r = R.next()
                        pe.wait(m, ex_ready, *misc.free)
                        mr = pe.put(mm(misc.ap[:, 0:SEQ], ex[:, g, :], s.rT.ap[:], True, True))
                        if g == 1:
                            s.rT.free = [mr]
                        yield
                        act.wait(mr, *r.free)
                        mc = act.put(nc.scalar.copy(r.ap[:], misc.ap[:, 0:SEQ]))
                        misc.free = [mc]
                        o = s.o32[g].ap[:, 0, :]
                        pool.wait(mc, s.O_ready[g])
                        m2 = pool.put(nc.gpsimd.tensor_tensor(o, o, r.ap[:], ALU.mult))
                        r.free = [m2]
                        ms = split(o, s.OT.ap[0][:, g, :], s.OT.ap[1][:, g, :], [m2], s.OT.free)
                        s.o32[g].free = ms
                        ready += ms
                        yield
                    pe.wait(*ready, *wo_ready, *misc.free)
                    for i in range(2):
                        rows = slice(i * P, (i + 1) * P)
                        for c in range(DC):
                            last = mm3(misc.ap[:, i * D:(i + 1) * D], (s.OT.ap[0][:, c, rows], s.OT.ap[1][:, c, rows]),
                                       [w[:, c, :] for w in wo], i == 0 and c == 0, c == DC - 1)
                    m = pe.put(last)
                    s.OT.free = [m]
                    dve.wait(m, *x_ready[b])
                    v = misc.ap[:, :].rearrange("p (t n) -> p t n", t=2)
                    m = dve.put(nc.vector.tensor_tensor(X[:, 2 * b:2 * b + 2, :], v, X[:, 2 * b:2 * b + 2, :], ALU.add))
                    misc.free = [m]
                    x_ready[b] = [m]
                    yield
                    for _ in out_of(b, m, misc):
                        yield

                N = BATCH * U
                for _ in value_project(0):
                    pass
                qk, pp = {0: qk_project(0, 0)}, {}
                side = tail = None
                for i in range(N + 1):
                    b, u = divmod(i, U)
                    if i + 1 < N:
                        b2, u2 = divmod(i + 1, U)
                        if u2 == 0 and side is not None:
                            for _ in side:
                                pass
                        qk[i + 1] = qk_project(b2, u2)
                    if i < N:
                        pp[i] = scores(b, u, qk[i])
                    if u == U - 3 and b + 1 < BATCH:
                        if tail is not None:
                            for _ in tail:
                                pass
                        side = value_project(b + 1)
                    if u >= U - 3:
                        advance(side, 2)
                    if i >= 1:
                        bp, up = divmod(i - 1, U)
                        xs = [turn(up, 0, pp[i - 1])]
                        for j in range(T):
                            if j + 1 < T:
                                xs.append(turn(up, j + 1, pp[i - 1]))
                            values(bp, up * T + j, xs[j])
                        advance(tail, 2)
                        if up == U - 1:
                            tail = finish(bp)
                            advance(tail)
                for _ in tail:
                    pass

        def norm_out(b, m, bank):
            ms = layer_norm(b, [m])
            yield
            yield
            to_xt(b, X[:, 2 * b:2 * b + 2, :], ms, bank)
            yield

        def from_xt(b):
            def parts_of(c, i, w):
                cols = tok(b) if i is None else slice(b * SEQ + i * P, b * SEQ + (i + 1) * P)
                hi, lo = XT_hi[:, c, cols], XT_lo[:, c, cols]
                return [(hi, w[0]), (hi, w[1]), (lo, w[0])]
            return xt_ready[b] or [], parts_of

        def cross_attention_0():
            with ExitStack() as sc:
                stage = alloc(sc, "b_ctx_stage", [P, BATCH * SEQ])
                parts = alloc(sc, "b_ctx", [P, BATCH * SEQ], F32R)
                packed = alloc(sc, "b_ctx_hi", [P, BATCH * SEQ], F32R)
                m = load(act, stage[:], t["ctxT"])
                act.wait(m)
                m = act.put(nc.scalar.copy(packed[:], stage[:]))
                dve.wait(m, *ready_c)
                m = dve.put(nc.vector.scalar_tensor_tensor(parts[:], packed[:].bitcast(F32), signs[:, 4:5], stage[:],
                                                           ALU.mult, ALU.add))

                def contraction(b):
                    def parts_of(c, i, w):
                        cols = tok(b) if i is None else slice(b * SEQ + i * P, b * SEQ + (i + 1) * P)
                        return [(parts[:, cols], w[0]), (parts[:, cols], w[1])]
                    return [m], parts_of

                narrow_attention("b", 16, 16, 16, ("b_wq", "b_wk", "b_wv", "b_wo"), contraction, 0, 1,
                                 "expand16", (XT_hi, XT_lo), norm_out)

        def experts(name, w_dram, gate_dram, capped, out_of):
            E, INTER = 8, 512
            IC = INTER // P
            HALF = 2 * SEQ
            with ExitStack() as sc:
                def A(n, *a, **k):
                    return alloc(sc, f"{name}_{n}", *a, **k)

                gate_stage = A("gate_stage", [P, DC, E])
                gate = [A(f"gate_{x}", [P, DC, E], F32R) for x in ("hi", "lo")]
                iota = A("iota", [P, E])
                m_iota = load(act, iota[:], t["iota8"])
                m = load(act, gate_stage[:], t[gate_dram])
                gate_ready = split(gate_stage[:], gate[0][:], gate[1][:], [m])
                stage = Ring([Buf(A(f"stage{i}", [P, 3 * DC * INTER])) for i in range(2)])
                W = Ring([Buf([A(f"w{i}_{x}", [P, 3 * DC * INTER], F32R) for x in ("hi", "lo")]) for i in range(2)])
                silu = Ring([Buf(A(f"silu{i}", [P, HALF])) for i in range(3)])
                h32 = Ring([Buf(A(f"h32_{i}", [P, HALF])) for i in range(3)])
                hT = Ring([Buf([A(f"hT{i}_{x}", [P, IC, HALF], F32R) for x in ("hi", "lo")]) for i in range(2)])
                logit = A("logit", [P, TILES, E])
                e_ = A("e", [P, TILES, E])
                wts = A("wts", [P, TILES, E])
                red = A("red", [P, 4, TILES])
                top = A("top", [P, TILES, 8])
                idx = A("idx", [P, TILES, 8], U32)
                idxf = A("idxf", [P, TILES, 8])

                gate_banks = Ring(psum[0:2])
                up_banks = Ring(psum[2:4])
                out_banks = Ring(psum[4:7])
                misc = psum[7]

                def prepare(e):
                    s, w = stage.next(), W.next()
                    sp.wait(*s.free)
                    m = load(sp, s.ap[:], t[w_dram][e])
                    n = s.ap.shape[1] // 3
                    w.ready = []
                    for c in range(3):
                        cols = slice(c * n, (c + 1) * n)
                        w.ready += split(s.ap[:, cols], w.ap[0][:, cols], w.ap[1][:, cols], [m], w.free)
                    s.free = w.ready
                    return w

                def route():
                    pe.wait(*gate_ready, *misc.free)
                    for n in range(TILES):
                        pe.wait(*(xt_ready[n // 2] or []))
                        cols = slice(n * P, (n + 1) * P)
                        for c in range(DC):
                            last = mm3(misc.ap[:, n * E:(n + 1) * E], (XT_hi[:, c, cols], XT_lo[:, c, cols]),
                                       [g[:, c, :] for g in gate], c == 0, c == DC - 1)
                    m = pe.put(last)
                    src = misc.ap[:, 0:TILES * E].rearrange("p (n e) -> p n e", e=E)
                    bc = lambda x: x.unsqueeze(2).broadcast_to([P, TILES, E])
                    if capped:
                        act.wait(m)
                        m = act.put(nc.scalar.activation(e_[:], src, ACT.Tanh, scale=1.0 / capped))
                        misc.free = [m]
                        dve.wait(m)
                        m = dve.put(nc.vector.tensor_scalar(logit[:], e_[:], float(capped), None, ALU.mult))
                    else:
                        dve.wait(m)
                        m = dve.put(nc.vector.tensor_copy(logit[:], src))
                        misc.free = [m]
                    dve.wait(m)
                    m = dve.put(nc.vector.tensor_reduce(red[:, 0, :], logit[:], AX.X, ALU.max))
                    dve.wait(m)
                    m = dve.put(nc.vector.tensor_tensor(e_[:], logit[:], bc(red[:, 0, :]), ALU.subtract))
                    act.wait(m)
                    m = act.put(nc.scalar.activation(e_[:], e_[:], ACT.Exp))
                    key = e_ if capped else logit
                    dve.wait(m)
                    if capped:
                        ms = [dve.put(nc.vector.tensor_reduce(red[:, 1, :], e_[:], AX.X, ALU.add))]
                    else:
                        ms = []
                    tops = [dve.put(nc.vector.max(top[:, n, :], key[:, n, :])) for n in range(TILES)]
                    dve.wait(tops[-1])
                    tops = [dve.put(nc.vector.max_index(idx[:, n, :], top[:, n, :], key[:, n, :]))
                            for n in range(TILES)]
                    dve.wait(tops[-1])
                    m = dve.put(nc.vector.tensor_copy(idxf[:], idx[:]))
                    dve.wait(m, m_iota)
                    ms2 = []
                    for n in range(TILES):
                        ms2.append(dve.put(nc.vector.tensor_scalar(wts[:, n, :], iota[:], idxf[:, n, 0:1], None,
                                                                   ALU.is_equal)))
                    dve.wait(ms2[-1])
                    for n in range(TILES):
                        m = dve.put(nc.vector.scalar_tensor_tensor(wts[:, n, :], iota[:], idxf[:, n, 1:2],
                                                                   wts[:, n, :], ALU.is_equal, ALU.add))
                    dve.wait(m)
                    m = dve.put(nc.vector.tensor_tensor(wts[:], wts[:], e_[:], ALU.mult))
                    if not capped:
                        dve.wait(m)
                        ms = [dve.put(nc.vector.tensor_reduce(red[:, 1, :], wts[:], AX.X, ALU.add))]
                    dve.wait(m, *ms)
                    m = dve.put(nc.vector.reciprocal(red[:, 2, :], red[:, 1, :]))
                    dve.wait(m)
                    return dve.put(nc.vector.tensor_tensor(wts[:], wts[:], bc(red[:, 2, :]), ALU.mult))

                def up(e, half, ic, w, h):
                    g, u = gate_banks.next(), up_banks.next()
                    cols = slice(half * HALF, (half + 1) * HALF)
                    pe.wait(*w.ready, *(xt_ready[2 * half] or []), *(xt_ready[2 * half + 1] or []))
                    n = DC * INTER
                    marks = []
                    for k, bank in enumerate((g, u)):
                        pe.wait(*bank.free)
                        for c in range(DC):
                            at = k * n + c * INTER + ic * P
                            last = mm3(bank.ap[:, :], [x[:, at:at + P] for x in w.ap],
                                       (XT_hi[:, c, cols], XT_lo[:, c, cols]), c == 0, c == DC - 1)
                        marks.append(pe.put(last))
                    if e == E - 1 and ic == IC - 1:
                        xt_read[2 * half].append(marks[1])
                        xt_read[2 * half + 1].append(marks[1])
                    s, y = silu.next(), h32.next()
                    act.wait(marks[0], *s.free)
                    m = act.put(nc.scalar.activation(s.ap[:], g.ap[:, :], ACT.Silu))
                    g.free = [m]
                    dve.wait(m, marks[1], *y.free)
                    m = dve.put(nc.vector.tensor_tensor(y.ap[:], u.ap[:, :], s.ap[:], ALU.mult))
                    u.free = s.free = [m]
                    y.free = split(y.ap[:], h.ap[0][:, ic, :], h.ap[1][:, ic, :], [m], h.free if ic == 0 else (),
                                   lo_on=dve)
                    h.ready += y.free

                def down(e, half, w, h, wts_ready):
                    n2 = 2 * DC * INTER
                    pe.wait(*h.ready)
                    for pair in range(2):
                        bank = out_banks.next()
                        pe.wait(*bank.free)
                        for i in range(2):
                            rows = slice((2 * pair + i) * P, (2 * pair + i + 1) * P)
                            for ic in range(IC):
                                cols = slice(n2 + ic * D, n2 + (ic + 1) * D)
                                last = mm3(bank.ap[:, i * D:(i + 1) * D], (h.ap[0][:, ic, rows], h.ap[1][:, ic, rows]),
                                           [x[:, cols] for x in w.ap], i == 0 and ic == 0, ic == IC - 1)
                        m = pe.put(last)
                        b = 2 * half + pair
                        ms = []
                        for i in range(2):
                            n = 2 * b + i
                            dve.wait(m, wts_ready, *x_ready[b])
                            ms.append(dve.put(nc.vector.scalar_tensor_tensor(
                                X[:, n, :], bank.ap[:, i * D:(i + 1) * D], wts[:, n, e:e + 1], X[:, n, :],
                                ALU.mult, ALU.add)))
                        bank.free = ms
                        x_ready[b] = ms
                        yield b, ms
                    h.free = [m]
                    if half == 1:
                        w.free = [m]

                w = {0: prepare(0)}
                wts_ready = route()
                pending = None
                tails = []
                for e in range(E):
                    for half in range(2):
                        h = hT.next()
                        h.ready = []
                        for ic in range(IC):
                            up(e, half, ic, w[e], h)
                            if pending is not None and ic in (0, 1):
                                got = next(pending, None)
                                if got and e == E - 1 and half == 1:
                                    tails.append(out_of(got[0], got[1], misc))
                            elif ic >= 2:
                                for x in tails:
                                    advance(x)
                        if pending is not None:
                            for _ in pending:
                                pass
                        if half == 0 and e + 1 < E:
                            w[e + 1] = prepare(e + 1)
                        pending = down(e, half, w[e], h, wts_ready)
                for b, ms in pending:
                    tails.append(out_of(b, ms, misc))
                for x in tails:
                    for _ in x:
                        pass

        def norm_out_many(b, ms, bank):
            r = layer_norm(b, ms)
            yield
            to_xt(b, X[:, 2 * b:2 * b + 2, :], r, bank)
            yield

        def latent_attention():
            H, QW, HALFQ = 16, 192, 96
            PIECE = 400
            with ExitStack() as sc:
                def A(n, *a, **k):
                    return alloc(sc, f"e_{n}", *a, **k)

                ropeq = A("ropeq", [HALFQ, 4, SEQ])
                m_ropeq = load(act, ropeq[:], t["ropeq"])
                KTb = [A(f"KT{b}", [P, CTX + 1], F32R) for b in range(BATCH)]
                kvb = [A(f"kv{b}", [P, KT, P], F32R) for b in range(BATCH)]
                kt_ready, kv_ready = [], []
                aux = psum[7]
                score = psum[0:4]
                tb = Ring(psum[4:6])
                ctx_bank = psum[6]

                with ExitStack() as pre:
                    def B(n, *a, **k):
                        return alloc(pre, f"e_{n}", *a, **k)
                    ropek = B("ropek", [P, 2, KT, LAT])
                    ctx_in = Ring([Buf(B(f"ctx{i}", [P, KT, LAT])) for i in range(2)])
                    turned = Ring([Buf(B(f"turned{i}", [P, KT, LAT])) for i in range(2)])
                    kvd = Ring([Buf(B(f"kvd{i}", [P, KT, 2, LAT])) for i in range(2)])
                    part = Ring([Buf(B(f"part{i}", [P, 512], F32R)) for i in range(2)])
                    m_ropek = load(sp, ropek[:], t["ropek"])
                    for b in range(BATCH):
                        x, r, k = ctx_in.next(), turned.next(), kvd.next()
                        sp.wait(*x.free)
                        m = load(sp, x.ap[:], t["ctx"][b])
                        pool.wait(m, m_ropek, *r.free)
                        ms = [pool.put(nc.gpsimd.tensor_tensor(r.ap[:, :, 0:32], x.ap[:, :, 32:64],
                                                               ropek[:, 1, :, 0:32], ALU.mult)),
                              pool.put(nc.gpsimd.tensor_tensor(r.ap[:, :, 32:64], x.ap[:, :, 0:32],
                                                               ropek[:, 1, :, 32:64], ALU.mult))]
                        dve.wait(*ms)
                        m = dve.put(nc.vector.tensor_tensor(x.ap[:], x.ap[:], ropek[:, 0, :, :], ALU.mult))
                        dve.wait(*k.free)
                        dve.wait(m)
                        ms = [dve.put(nc.vector.tensor_tensor(k.ap[:, :, i, :], x.ap[:], r.ap[:], ALU.add))
                              for i in range(2)]
                        x.free = r.free = ms
                        hi, lo = kvb[b][:, :, 0:LAT], kvb[b][:, :, LAT:P]
                        kv_ready.append(split(k.ap[:, :, 0, :], hi, lo, ms, lo_on=pool))
                        pe.wait(*ms)
                        ready = [act.put(nc.scalar.copy(KTb[b][:, CTX:CTX + 1], signs[:, 7:8]))]
                        for g in range(0, KT, 4):
                            bank, pt = tb.next(), part.next()
                            pe.wait(*bank.free)
                            n = min(4, KT - g)
                            width = min(CTX - g * P, n * P)
                            for i in range(n):
                                rows = min(P, CTX - (g + i) * P)
                                last = nc.tensor.transpose(
                                    bank.ap[:, i * P:i * P + rows],
                                    k.ap[0:rows, g + i, :, :].rearrange("p a d -> p (a d)"), ident[0:rows, 0:rows])
                            mt = pe.put(last)
                            act.wait(mt, *pt.free)
                            m1 = act.put(nc.scalar.copy(pt.ap[:, 0:width], bank.ap[:, 0:width]))
                            dve.wait(m1)
                            m2 = dve.put(nc.vector.scalar_tensor_tensor(
                                KTb[b][:, g * P:g * P + width], pt.ap[:, 0:width].bitcast(F32), signs[:, 4:5],
                                bank.ap[:, 0:width], ALU.mult, ALU.add))
                            bank.free = pt.free = [m2]
                            ready.append(m2)
                        k.free = [mt] + kv_ready[-1]
                        kt_ready.append(ready)
                    drained = kt_ready[-1] + kv_ready[-1] + kt_ready[-2] + kv_ready[-2]

                stage = Ring([Buf(A(f"stage{i}", [P, 832])) for i in range(2)])
                stage_r = Ring([Buf(A(f"stage_r{i}", [LAT, 320])) for i in range(2)])
                wq = Ring([Buf([A(f"wq{i}_{x}", [P, DC, QW], F32R) for x in ("hi", "lo")]) for i in range(2)])
                w2 = Ring([Buf([A(f"w2{i}_{x}", [HALFQ, 2, P], F32R) for x in ("hi", "lo")]) for i in range(2)])
                wf = Ring([Buf([A(f"wf{i}_{x}", [P, D], F32R) for x in ("hi", "lo")]) for i in range(2)])
                r0 = Ring([Buf(A(f"r0_{i}", [HALFQ, 2, SEQ])) for i in range(2)])
                r1 = Ring([Buf(A(f"r1_{i}", [HALFQ, 2, SEQ])) for i in range(2)])
                r2 = Ring([Buf(A(f"r2_{i}", [HALFQ, 2, SEQ])) for i in range(2)])
                qr = Ring([Buf([A(f"qr{i}_{x}", [HALFQ, 2, SEQ], F32R) for x in ("hi", "lo")]) for i in range(2)])
                qk = Ring([Buf([A(f"qk{i}_{x}", [P, SEQ], F32R) for x in ("hi", "lo")]) for i in range(2)])
                Pm = Ring([Buf(A(f"P{i}", [P, 2, CTX])) for i in range(2)])
                PT = Ring([Buf([A(f"PT{i}_{x}", [P, 2, SEQ], F32R) for x in ("hi", "lo")]) for i in range(3)])
                st = Ring([Buf(A(f"st{i}", [P, 2, 8])) for i in range(4)])
                cx = Ring([Buf([A(f"cx{i}_{x}", [P, SEQ], F32R) for x in ("hi", "lo")]) for i in range(2)])
                sp.wait(*drained)
                act.wait(*drained)
                dve.wait(*drained)
                pool.wait(*drained)

                def prepare(h):
                    s, r = stage.next(), stage_r.next()
                    sp.wait(*s.free, *r.free)
                    m, mr = load(sp, s.ap[:], t["e_w"][h]), load(sp, r.ap[:], t["e_wr"][h])
                    yield
                    q = wq.next()
                    pe.wait(m, *aux.free)
                    for c in range(DC):
                        last = mm(aux.ap[:, c * QW:(c + 1) * QW], s.ap[:, c * P:(c + 1) * P], s.ap[:, D:D + QW],
                                  True, True)
                    m0 = pe.put(last)
                    v = aux.ap[:, 0:DC * QW].rearrange("p (c n) -> p c n", c=DC)
                    q.ready = aux.free = split(v, q.ap[0][:], q.ap[1][:], [m0], q.free, lo_on=dve)
                    yield
                    a = w2.next()
                    pe.wait(mr, *aux.free)
                    for c in range(2):
                        last = mm(aux.ap[0:HALFQ, c * P:(c + 1) * P], r.ap[:, c * HALFQ:(c + 1) * HALFQ],
                                  r.ap[:, QW:QW + P], True, True)
                    m1 = pe.put(last)
                    v = aux.ap[0:HALFQ, 0:2 * P].rearrange("p (c n) -> p c n", c=2)
                    a.ready = aux.free = split(v, a.ap[0][:], a.ap[1][:], [m1], a.free, lo_on=dve)
                    r.free = [m1]
                    yield
                    f = wf.next()
                    pe.wait(*aux.free)
                    m2 = pe.put(mm(aux.ap[:, 0:D], s.ap[:, 704:832], s.ap[:, 448:704], True, True))
                    f.ready = aux.free = split(aux.ap[:, 0:D], f.ap[0][:], f.ap[1][:], [m2], f.free, lo_on=dve)
                    s.free = [m2]
                    hw[h] = (q, a, f)
                    yield

                hw = {}

                class Unit:
                    pass

                def queries(u):
                    q, a, _ = hw[u.h]
                    cols = tok(u.b)
                    pe.wait(*q.ready, *(xt_ready[u.b] or []), *aux.free)
                    for c in range(2):
                        for d in range(DC):
                            last = mm3(aux.ap[0:HALFQ, c * SEQ:(c + 1) * SEQ],
                                       [w[:, d, c * HALFQ:(c + 1) * HALFQ] for w in q.ap],
                                       (XT_hi[:, d, cols], XT_lo[:, d, cols]), d == 0, d == DC - 1)
                    m = pe.put(last)
                    if u.h == H - 1:
                        xt_read[u.b].append(m)
                    if u.b == BATCH - 1:
                        q.free = [m]
                    y, x1, x2, z = r0.next(), r1.next(), r2.next(), qr.next()
                    act.wait(m, *y.free)
                    v = y.ap
                    m = act.put(nc.scalar.copy(v[:].rearrange("p c n -> p (c n)"), aux.ap[0:HALFQ, :]))
                    aux.free = [m]
                    pool.wait(m, m_ropeq, *x1.free, *x2.free)
                    ms = [pool.put(nc.gpsimd.tensor_tensor(x1.ap[:], v[:], ropeq[:, 0:2, :], ALU.mult))]
                    for c in range(2):
                        ms.append(pool.put(nc.gpsimd.tensor_tensor(x2.ap[:, c, :], v[:, 1 - c, :],
                                                                   ropeq[:, 2 + c, :], ALU.mult)))
                    y.free = ms
                    pool.wait(*ms)
                    m = pool.put(nc.gpsimd.tensor_tensor(x1.ap[:], x1.ap[:], x2.ap[:], ALU.add))
                    x2.free = [m]
                    u.z, u.z_sum = z, m
                    u.x1 = x1
                    yield
                    z.ready = x1.free = split(x1.ap[:], z.ap[0][:], z.ap[1][:], [m], z.free)
                    yield
                    k = qk.next()
                    pe.wait(*z.ready, *a.ready, *aux.free)
                    for c in range(2):
                        last = mm3(aux.ap[:, 0:SEQ], [w[:, c, :] for w in a.ap],
                                   (z.ap[0][:, c, :], z.ap[1][:, c, :]), c == 0, c == 1)
                    m = pe.put(last)
                    z.free = [m]
                    if u.b == BATCH - 1:
                        a.free = [m]
                    k.ready = split(aux.ap[:, 0:SEQ], k.ap[0][:], k.ap[1][:], [m], k.free, lo_on=dve)
                    aux.free = k.ready
                    u.qk = k
                    yield

                def scores(u, i):
                    k = u.qk
                    pe.wait(*k.ready, *kt_ready[u.b])
                    rows = slice(i * P, (i + 1) * P)
                    ms = []
                    for j in range(4):
                        pe.wait(*score[j].free)
                        for n in range(2):
                            last = mm(score[j].ap[:, 0:PIECE + 2], k.ap[n][:, rows],
                                      KTb[u.b][:, j * PIECE:j * PIECE + PIECE + 2], n == 0, n == 1)
                        ms.append(pe.put(last))
                    if i == 1:
                        k.free = [ms[-1]]
                    s = u.st
                    dve.wait(ms[0], *s.free)
                    mx = []
                    for j in range(4):
                        dve.wait(ms[j])
                        mx.append(dve.put(nc.vector.tensor_reduce(s.ap[:, i, j:j + 1], score[j].ap[:, 0:PIECE + 1],
                                                                  AX.X, ALU.max)))
                    dve.wait(*mx)
                    u.neg[i] = dve.put(nc.vector.tensor_reduce(s.ap[:, i, 4:5], s.ap[:, i, 0:4], AX.X, ALU.max,
                                                               negate=True))

                def exponentials(u, i, js):
                    s, p = u.st, u.p
                    act.wait(u.neg[i], *(p.free if i == 0 else ()))
                    ms = []
                    for j in js:
                        n = PIECE + (j == 3)
                        m = act.put(nc.scalar.activation(
                            p.ap[:, i, j * PIECE:j * PIECE + n], score[j].ap[:, 0:n], ACT.Exp, bias=s.ap[:, i, 4:5],
                            accum_out=s.ap[:, i, j:j + 1]))
                        score[j].free = [m]
                        ms.append(m)
                    p.ready += ms

                def row_sums(u, i):
                    s = u.st
                    dve.wait(*u.p.ready)
                    m = dve.put(nc.vector.tensor_reduce(s.ap[:, i, 5:6], s.ap[:, i, 0:4], AX.X, ALU.add))
                    dve.wait(m)
                    u.r_ready.append(dve.put(nc.vector.reciprocal(s.ap[:, i, 6:7], s.ap[:, i, 5:6])))

                GROUPS = -(-KT // 2)

                def turn(u, g):
                    bank, x = tb.next(), PT.next()
                    pe.wait(*u.p.ready, *bank.free)
                    n = min(2, KT - 2 * g)
                    rows = min(P, CTX - 2 * g * P)
                    for c in range(n):
                        k0 = (2 * g + c) * P
                        for i in range(2):
                            last = nc.tensor.transpose(bank.ap[0:rows, c * SEQ + i * P:c * SEQ + (i + 1) * P],
                                                       u.p.ap[:, i, k0:k0 + rows], ident[:])
                    m = pe.put(last)
                    if g == GROUPS - 1:
                        u.p.free = [m]
                    v = bank.ap[0:rows, 0:n * SEQ].rearrange("p (c n) -> p c n", c=n)
                    x.ready = split(v, x.ap[0][0:rows, 0:n, :], x.ap[1][0:rows, 0:n, :], [m], x.free, lo_on=dve)
                    bank.free = x.ready
                    return x, n, rows

                def attend(u, g, got):
                    x, n, rows = got
                    if g == 0:
                        pe.wait(*ctx_bank.free)
                    pe.wait(*x.ready, *kv_ready[u.b])
                    for c in range(n):
                        w = kvb[u.b][0:rows, 2 * g + c, :]
                        for y in range(2):
                            last = mm(ctx_bank.ap[:, 0:SEQ], w, x.ap[y][0:rows, c, :],
                                      g == 0 and c == 0 and y == 0, g == GROUPS - 1 and c == n - 1 and y == 1)
                    m = pe.put(last)
                    x.free = [m]
                    if g == GROUPS - 1:
                        c = u.cx = cx.next()
                        c.ready = split(ctx_bank.ap[:, 0:SEQ], c.ap[0][:], c.ap[1][:], [m], c.free, lo_on=dve)
                        ctx_bank.free = c.ready

                def project_out(u):
                    c, f = u.cx, hw[u.h][2]
                    pe.wait(*c.ready, *f.ready, *aux.free)
                    for i in range(2):
                        rows = slice(i * P, (i + 1) * P)
                        last = mm3(aux.ap[:, i * D:(i + 1) * D], (c.ap[0][:, rows], c.ap[1][:, rows]),
                                   [w[:] for w in f.ap], True, True)
                    m = pe.put(last)
                    c.free = [m]
                    if u.b == BATCH - 1:
                        f.free = [m]
                    ms = []
                    for i in range(2):
                        n = 2 * u.b + i
                        dve.wait(m, u.r_ready[i], *x_ready[u.b])
                        ms.append(dve.put(nc.vector.scalar_tensor_tensor(
                            X[:, n, :], aux.ap[:, i * D:(i + 1) * D], u.st.ap[:, i, 6:7], X[:, n, :],
                            ALU.mult, ALU.add)))
                    aux.free = u.st.free = ms
                    x_ready[u.b] = ms

                N = H * BATCH
                units = []
                for _ in prepare(0):
                    pass

                def begin(i):
                    u = Unit()
                    u.h, u.b = divmod(i, BATCH)
                    u.st, u.neg, u.r_ready = st.next(), {}, []
                    units.append(u)
                    return queries(u)

                for _ in begin(0):
                    pass
                nxt = prep = None
                for i in range(N + 2):
                    u = units[i] if i < N else None
                    v = units[i - 1] if 0 <= i - 1 < N else None
                    w = units[i - 2] if 0 <= i - 2 < N else None
                    nxt = begin(i + 1) if i + 1 < N else None
                    got = {}

                    def turn_(g):
                        if v is not None:
                            got[g] = turn(v, g)

                    def attend_(g):
                        if v is not None:
                            attend(v, g, got[g])

                    if u is not None:
                        u.p = Pm.next()
                        u.p.ready = []
                        scores(u, 0)
                    turn_(0)
                    turn_(1)
                    advance(nxt)
                    if u is not None:
                        exponentials(u, 0, (0, 1))
                    attend_(0)
                    turn_(2)
                    if u is not None:
                        exponentials(u, 0, (2, 3))
                    attend_(1)
                    turn_(3)
                    attend_(2)
                    if u is not None:
                        scores(u, 1)
                        row_sums(u, 0)
                    if w is not None:
                        project_out(w)
                    turn_(4)
                    attend_(3)
                    advance(nxt)
                    if u is not None:
                        exponentials(u, 1, (0, 1))
                    turn_(5)
                    attend_(4)
                    if u is not None:
                        exponentials(u, 1, (2, 3))
                    advance(nxt)
                    turn_(6)
                    attend_(5)
                    if u is not None:
                        row_sums(u, 1)
                    if i % BATCH == 0 and i // BATCH + 1 < H:
                        prep = prepare(i // BATCH + 1)
                    if i % BATCH < 3:
                        advance(prep, 1 + (i % BATCH == 0))
                    attend_(6)
                tails = [norm_out_many(b, x_ready[b], aux) for b in range(BATCH)]
                for k in range(3):
                    for x in tails:
                        advance(x)

        ln_w = vec("ln_w", [P, 2 * DC])
        m_ln = load(sp, ln_w[:], t["f_ln"])

        def rms_to_xt(b, marks, bank, weight):
            T, y32 = tiny.next(), normed.next()
            m = row_stats(b, T, marks)
            st_ = T.ap[:, 12:16].rearrange("p (t s) -> p t s", s=2)
            v, y, s = T.ap[:, 16:18], T.ap[:, 18:20], T.ap[:, 20:22]
            dve.wait(m)
            m = dve.put(nc.vector.tensor_tensor(s, st_[:, :, 0], st_[:, :, 0], ALU.mult))
            dve.wait(m)
            m = dve.put(nc.vector.scalar_tensor_tensor(v, s, EPS, st_[:, :, 1], ALU.add, ALU.add))
            m = inv_sqrt(v, y, s, [m])
            dve.wait(m, *y32.free)
            ms = [dve.put(nc.vector.tensor_scalar(y32.ap[:, i, :], X[:, 2 * b + i, :], T.ap[:, 18 + i:19 + i], None,
                                                  ALU.mult)) for i in range(2)]
            T.free = ms
            yield
            act.wait(m_ln)
            dve.wait(m_ln)
            y32.free = [to_xt(b, y32.ap, ms, bank, weight)]
            yield

        def last_block():
            x_in = alloc(top, "x_in", [P, TILES, D])
            first, second = ln_w[:, 0:DC], ln_w[:, DC:2 * DC]
            x_in_ready = [act.put(nc.scalar.copy(x_in[:, 2 * b:2 * b + 2, :], X[:, 2 * b:2 * b + 2, :]))
                          for b in range(BATCH) if not act.wait(*x_ready[b])]

            def middle(b, m, bank):
                for _ in rms_to_xt(b, [m], bank, second):
                    yield
                pair = X[:, 2 * b:2 * b + 2, :]
                dve.wait(x_in_ready[b], *x_ready[b])
                x_ready[b] = [dve.put(nc.vector.tensor_tensor(pair, pair, x_in[:, 2 * b:2 * b + 2, :], ALU.add))]
                yield

            gens = [rms_to_xt(b, x_ready[b], psum[7], first) for b in range(BATCH)]
            for g in gens:
                for _ in g:
                    pass
            narrow_attention("f", 16, 16, 16, ("f_wq", "f_wk", "f_wv", "f_wo"), from_xt, 0, 1, "expand16",
                             (XT_hi, XT_lo), middle)
            settle()
            experts("g", "g_w", "g_gate", None, store_out)

        def store_out(b, ms, bank):
            r = layer_norm(b, ms)
            sp.wait(*r)
            stores.append(load(sp, out.rearrange("(n p) d -> p n d", p=P)[:, 2 * b:2 * b + 2, :],
                               X[:, 2 * b:2 * b + 2, :]))
            yield

        layer0_attention()
        settle()
        cross_attention_0()
        settle()
        experts("c", "c_w", "c_gate", 30.0, norm_out_many)
        settle()
        narrow_attention("d", 8, 32, 8, ("d_wq", "d_wk", "d_wv", "d_wo"), from_xt, 2, 3, "expand8",
                         (XT_hi, XT_lo), norm_out)
        settle()
        latent_attention()
        settle()
        last_block()

        sp.wait(*stores)


def tables():
    import numpy as np
    f = np.float32
    k, q = np.arange(P)[None, :], np.arange(P)[:, None]
    cut = lambda keep: np.where(keep, 0, MASKED).astype(f)
    j = np.arange(192)[None, :]
    masks = np.concatenate([cut((k <= q) & (q - k <= 64)), cut((q <= j) & (j <= q + 64)), cut(k <= q)], 1)
    p = np.arange(P)
    signs = np.zeros((P, 8), f)
    signs[:, 0] = -((p % 64) >= 32).astype(f)
    signs[:, 1] = -((p // 16) % 2).astype(f)
    signs[:, 2] = -((p % 32) >= 16).astype(f)
    signs[:, 3] = -((p // 8) % 2).astype(f)
    signs[:, 4] = -(p >= 64).astype(f)
    half = 64
    inv = (f(1.0) / np.power(f(10000.0), np.arange(half, dtype=f) / f(half))).astype(f)
    fr = (np.arange(SEQ, dtype=f)[None, :] * inv[:, None]).astype(f)
    cos, sin = np.cos(fr).astype(f), np.sin(fr).astype(f)
    rope0 = np.stack([np.concatenate([cos, cos]), np.concatenate([sin, -sin])], 1)

    def latent(length, dim):
        inv = (f(1.0) / np.power(f(10000.0), np.arange(0, dim, 2, dtype=f) / f(dim))).astype(f)
        fr = (np.arange(length, dtype=f)[:, None] * inv[None, :]).astype(f)
        return np.repeat(np.sin(fr).astype(f), 2, -1), np.repeat(np.cos(fr).astype(f), 2, -1)

    sq, cq = latent(SEQ, 192)
    ropeq = np.stack([cq[:, :96].T, cq[:, 96:].T, -sq[:, :96].T, sq[:, 96:].T], 1)
    sk, ck = latent(CTX, LAT)
    sk = np.concatenate([-sk[:, :32], sk[:, 32:]], 1)
    pad = np.zeros((KT * P - CTX, LAT), f)
    ropek = np.stack([np.concatenate([a, pad]).reshape(KT, P, LAT).transpose(1, 0, 2) for a in (ck, sk)], 1)
    d = np.arange(D).reshape(2, 1, P)
    e16 = (np.arange(16)[None, :, None] == d // 16).astype(f).transpose(1, 0, 2)
    e8 = (np.arange(32)[None, :, None] == d // 8).astype(f).transpose(1, 0, 2)
    return {"ident": np.eye(P, dtype=f), "masks": masks, "signs": signs, "rope0": rope0,
            "ropeq": ropeq, "ropek": ropek, "expand16": e16, "expand8": e8,
            "iota8": np.tile(np.arange(8, dtype=f), (P, 1))}


def layouts(i):
    import numpy as np

    def rows(w):
        return w.reshape(w.shape[0] // P, P, w.shape[1]).transpose(1, 0, 2)

    def repeat_heads(w, hd, per_tile, shared=1):
        h = w.reshape(w.shape[0], -1, 1, hd)
        h = np.repeat(h, shared, axis=1)
        return np.broadcast_to(h, (w.shape[0], h.shape[1], 4, hd)).reshape(w.shape[0], -1)

    a = {}
    x = i["x"].reshape(BATCH * SEQ, D)
    a["x"], a["xT"] = x, x.T
    ctx = i["ctx_512"]
    pad = np.zeros((BATCH, KT * P - CTX, LAT), ctx.dtype)
    a["ctx"] = np.concatenate([ctx, pad], 1).reshape(BATCH, KT, P, LAT).transpose(0, 2, 1, 3)
    ct = ctx[:, :SEQ].transpose(2, 0, 1).reshape(LAT, BATCH * SEQ)
    a["ctxT"] = np.concatenate([ct, ct])
    a["a_wkv"] = rows(np.concatenate([i["L0_attn_wk"].T, i["L0_attn_wv"].T], 1)).reshape(P, -1)
    wq = rows(i["L0_attn_wq"].T).reshape(P, DC, 2, 2, 512)
    a["a_wq"] = wq.transpose(2, 0, 3, 1, 4).reshape(2, P, 2048)
    wo = i["L0_attn_wo"].T.reshape(2, 8, P, D)
    a["a_wo"] = wo.transpose(0, 2, 1, 3).reshape(2, P, 2048)
    wk, wv = i["L0_xattn_Wkv_expand"][:D].T, i["L0_xattn_Wkv_expand"][D:].T
    a["b_wq"] = rows(repeat_heads(i["L0_xattn_Wq"].T, 16, 2))
    a["b_wk"] = np.concatenate([repeat_heads(wk, 16, 2)] * 2)[:, None, :]
    a["b_wv"] = np.concatenate([wv] * 2)[:, None, :]
    a["b_wo"] = rows(i["L0_xattn_Wout"].T)
    a["d_wq"] = rows(repeat_heads(i["L1_attn_Wq"], 8, 4))
    a["d_wk"] = rows(repeat_heads(i["L1_attn_Wk"], 8, 4, shared=4))
    a["d_wv"] = rows(i["L1_attn_Wv"])
    a["d_wo"] = rows(i["L1_attn_Wo"])
    a["f_wq"] = rows(repeat_heads(i["L1_ffn_Wq"].T, 16, 2))
    a["f_wk"] = rows(repeat_heads(i["L1_ffn_Wk"].T, 16, 2))
    a["f_wv"] = rows(i["L1_ffn_Wv"].T)
    a["f_wo"] = rows(i["L1_ffn_Wo"].T)
    a["f_ln"] = np.concatenate([rows(i["L1_ffn_w_ln1"][:, None])[:, :, 0], rows(i["L1_ffn_w_ln2"][:, None])[:, :, 0]], 1)
    def experts(w1, w3, w2):
        pack = lambda w, n: w.reshape(8, n, P, -1).transpose(0, 2, 1, 3).reshape(8, P, -1)
        return np.concatenate([pack(w1, DC), pack(w3, DC), pack(w2, 4)], 2)
    a["c_w"] = experts(i["L0_ffn_w1"], i["L0_ffn_w3"], i["L0_ffn_w2"])
    a["c_gate"] = rows(i["L0_ffn_w_gate"])
    a["g_w"] = experts(i["L1_ffn_Wg"].transpose(0, 2, 1), i["L1_ffn_Wu"].transpose(0, 2, 1),
                       i["L1_ffn_Wd"].transpose(0, 2, 1))
    a["g_gate"] = rows(i["L1_ffn_Wr"].T)
    wq = i["L1_xattn_Wq"].reshape(16, P, D)
    wo = i["L1_xattn_Wo"].T.reshape(16, P, D)
    kv = i["L1_xattn_w_kc_kv"]
    a["e_w"] = np.concatenate([wq, i["L1_xattn_w_kc_q"], wo, kv, kv], 2)
    kr = i["L1_xattn_W_kr"].transpose(0, 2, 1)
    a["e_wr"] = np.concatenate([i["L1_xattn_W_qr"].transpose(0, 2, 1), kr, kr], 2)
    return {k: np.ascontiguousarray(v) for k, v in a.items()}


def kernel(**inputs):
    import numpy as np
    import concourse.bacc as bacc
    from concourse.bass_utils import run_bass_kernel_spmd

    nc = bacc.Bacc("TRN2", target_bir_lowering=False, num_devices=1)
    arrays = {**layouts({k: np.asarray(v) for k, v in inputs.items()}), **tables()}
    t = {k: nc.dram_tensor("in_" + k, v.shape, mybir.dt.from_np(v.dtype), kind="ExternalInput").ap()
         for k, v in arrays.items()}
    out = nc.dram_tensor("out", (BATCH * SEQ, D), F32, kind="ExternalOutput").ap()
    decoder(nc, t, out)
    r = run_bass_kernel_spmd(nc, [{"in_" + k: v for k, v in arrays.items()}], core_ids=[0])
    return r.results[0]["out"].reshape(BATCH, SEQ, D)
```

```python
from contextlib import ExitStack

import concourse.bass as bass
from concourse import mybir

F32 = mybir.dt.float32
F32R = mybir.dt.float32r
BF16 = mybir.dt.bfloat16
I32 = mybir.dt.int32
U32 = mybir.dt.uint32
ALU = mybir.AluOpType
ACT = mybir.ActivationFunctionType
AX = mybir.AxisListType

P = 128
BATCH, SEQ, D = 4, 256, 256
TILES = BATCH * SEQ // P
DC = D // P
CTX, LAT = 1601, 64
KT = -(-CTX // P)
EPS = 1e-5
MASKED = -1e30


class Queue:

    def __init__(self, engine, sem):
        self.engine, self.sem, self.count, self.passed = engine, sem, 0, {}

    def put(self, instruction):
        instruction.then_inc(self.sem, 1)
        self.count += 1
        return (self.sem, self.count)

    def wait(self, *marks):
        for m in marks:
            if m is None:
                continue
            if isinstance(m, list):
                self.wait(*m)
                continue
            sem, value = m
            if self.passed.get(id(sem), 0) < value:
                self.engine.wait_ge(sem, value)
                self.passed[id(sem)] = value


class Buf:

    def __init__(self, ap):
        self.ap, self.readers, self.ready, self.held = ap, [], None, False

    @property
    def free(self):
        return self.readers

    @free.setter
    def free(self, marks):
        self.readers, self.held = marks, False


class Ring:

    def __init__(self, bufs):
        self.bufs, self.at = bufs, -1

    def next(self):
        self.at += 1
        b = self.bufs[self.at % len(self.bufs)]
        assert not b.held, "its last use has not named its readers yet"
        b.held = True
        return b


def decoder(nc, t, out):
    with ExitStack() as top:
        def sem(name):
            return top.enter_context(nc.semaphore(name))

        pe = Queue(nc.tensor, sem("pe_done"))
        act = Queue(nc.scalar, sem("act_done"))
        dve = Queue(nc.vector, sem("dve_done"))
        pool = Queue(nc.gpsimd, sem("pool_done"))
        sp = Queue(nc.sync, sem("sp_unused"))
        dma_sems = [sem(f"dma_{i}") for i in range(48)]
        dma_uses = [0] * len(dma_sems)
        dma_at = [0]

        def load(queue, dst, src):
            i = dma_at[0] % len(dma_sems)
            dma_at[0] += 1
            dma_uses[i] += 16
            queue.engine.dma_start(dst, src).then_inc(dma_sems[i], 16)
            return (dma_sems[i], dma_uses[i])

        def alloc(scope, name, shape, dtype=F32):
            return scope.enter_context(nc.sbuf_tensor(name, shape, dtype))

        psum = [Buf(top.enter_context(nc.psum_tensor(f"bank{i}", [P, 512], F32))) for i in range(8)]

        def vec(*a, **k):
            return alloc(top, *a, **k)

        ident = vec("ident", [P, P])
        ident_b = vec("ident_b", [P, P], BF16)
        mask_b = vec("mask_b", [P, 448], BF16)
        signs = vec("signs", [P, 8])
        ready_c = []

        def load_constants(mask_f):
            ready_c.extend([load(sp, ident[:], t["ident"]), load(sp, signs[:], t["signs"]),
                            load(sp, mask_f[:], t["masks"])])

        X = vec("X", [P, TILES, D])
        XT_hi = vec("XT_hi", [P, DC, BATCH * SEQ], F32R)
        XT_lo = vec("XT_lo", [P, DC, BATCH * SEQ], F32R)
        x_loaded = []
        window0, window1, causal = mask_b[:, 0:128], mask_b[:, 128:320], mask_b[:, 320:448]

        xt_ready = [None] * BATCH
        xt_read = [[] for _ in range(BATCH)]
        x_ready = [x_loaded for _ in range(BATCH)]

        def mm(o, a, b, start, stop):
            return nc.tensor.matmul(o, a, b, start=start, stop=stop, skip_group_check=True)

        def mm3(o, a, b, start, stop):
            mm(o, a[0], b[0], start, False)
            mm(o, a[0], b[1], False, False)
            return mm(o, a[1], b[0], False, stop)

        def tok(b, n=2):
            return slice(b * SEQ, b * SEQ + n * P)

        def split(src, hi, lo, marks, free=(), hi_on=act, lo_on=pool):
            hi_on.wait(*marks, *free)
            if hi_on is act:
                m1 = act.put(nc.scalar.copy(hi, src))
            else:
                m1 = hi_on.put(hi_on.engine.tensor_copy(hi, src))
            lo_on.wait(*marks, *free, m1)
            m2 = lo_on.put(lo_on.engine.tensor_tensor(lo, src, hi.bitcast(F32), ALU.subtract))
            return [m1, m2]

        tiny = Ring([Buf(vec(f"tiny{i}", [P, 64])) for i in range(2 * BATCH)])

        STEPS_OF_NORM = 4

        def inv_sqrt(v, y, s, marks):
            dve.wait(*marks)
            m = dve.put(nc.vector.tensor_single_scalar(s.bitcast(I32), v.bitcast(I32), 1,
                                                       ALU.logical_shift_right))
            dve.wait(m)
            m = dve.put(nc.vector.tensor_scalar(y.bitcast(I32), s.bitcast(I32), -1.0,
                                                float(0x5F3759DF), ALU.mult, ALU.add))
            for _ in range(3):
                yield
                dve.wait(m)
                m = dve.put(nc.vector.scalar_tensor_tensor(s, y, -0.5, y, ALU.mult, ALU.mult))
                dve.wait(m)
                m = dve.put(nc.vector.tensor_tensor(s, s, v, ALU.mult))
                dve.wait(m)
                m = dve.put(nc.vector.scalar_tensor_tensor(y, s, 1.5, y, ALU.add, ALU.mult))
            return m

        def row_stats(b, T, marks):
            ms = []
            dve.wait(*marks, *T.free)
            for i in range(2):
                ms.append(dve.put(nc.vector.bn_stats(T.ap[:, 6 * i:6 * i + 6], X[:, 2 * b + i, :])))
            dve.wait(*ms)
            for i in range(2):
                m = dve.put(nc.vector.bn_aggr(T.ap[:, 12 + 2 * i:14 + 2 * i], T.ap[:, 6 * i:6 * i + 6]))
            return m

        def layer_norm(b, marks):
            T = tiny.next()
            m = row_stats(b, T, marks)
            st = T.ap[:, 12:16].rearrange("p (t s) -> p t s", s=2)
            v, y, s = T.ap[:, 16:18], T.ap[:, 18:20], T.ap[:, 20:22]
            dve.wait(m)
            m = dve.put(nc.vector.tensor_scalar(v, st[:, :, 1], EPS, None, ALU.add))
            m = yield from inv_sqrt(v, y, s, [m])
            dve.wait(m)
            ms = []
            for i in range(2):
                ms.append(dve.put(nc.vector.tensor_scalar(
                    X[:, 2 * b + i, :], X[:, 2 * b + i, :], T.ap[:, 12 + 2 * i:13 + 2 * i],
                    T.ap[:, 18 + i:19 + i], ALU.subtract, ALU.mult)))
            T.free = ms
            x_ready[b] = ms
            yield

        def to_xt(b, src, marks, bank, weight=None):
            pe.wait(*marks, *bank.free, *ready_c)
            view = bank.ap[:, :].rearrange("p (c t) -> p c t", c=DC)
            for i in range(2):
                for c in range(DC):
                    last = nc.tensor.transpose(view[:, c, i * P:(i + 1) * P],
                                               src[:, i, c * P:(c + 1) * P], ident[:])
            m = pe.put(last)
            hi, lo = XT_hi[:, :, tok(b)], XT_lo[:, :, tok(b)]
            act.wait(m, *xt_read[b])
            dve.wait(m, *xt_read[b])
            if weight is None:
                m1 = act.put(nc.scalar.copy(hi, view))
                dve.wait(m1)
                m2 = dve.put(nc.vector.tensor_tensor(lo, view, hi.bitcast(F32), ALU.subtract))
                ms = [m1, m2]
            else:
                w = [weight[:, c:c + 1] for c in range(DC)]
                ms = [act.put(nc.scalar.activation(hi[:, c, :], view[:, c, :], ACT.Copy, scale=w[c]))
                      for c in range(DC)]
                dve.wait(*ms)
                ms += [dve.put(nc.vector.scalar_tensor_tensor(
                    lo[:, c, :], view[:, c, :], w[c], hi[:, c, :].bitcast(F32), ALU.mult, ALU.subtract))
                    for c in range(DC)]
            bank.free = ms
            xt_ready[b] = ms
            xt_read[b] = []
            return m

        def advance(g, n=1):
            for _ in range(n):
                if g is not None:
                    next(g, None)

        carried = {}

        def advance_carried():
            for g in carried.values():
                advance(g)

        def finish_carried(b):
            for _ in carried.pop(b, ()):
                pass

        landing = Buf(None)
        landed = {}

        def prefetch(phase):
            what = {
                "b": [(t["b_wq"], 0), (t["b_wk"], 2048)],
                "c": [(t["c_w"][0], 0), (t["c_gate"], 3072)],
                "d": [(t["d_wq"], 0), (t["d_wk"], 2048)],
                "e": [(t["ropek"], 0), (t["ctx"][0], 2 * KT * LAT), (t["ctx"][1], 3 * KT * LAT)],
                "f": [(t["f_wq"], 0), (t["f_wk"], 2048)],
                "g": [(t["g_w"][0], 0), (t["g_gate"], 3072)],
            }[phase]
            sp.wait(*landing.free)
            landed[phase] = []
            for src, at in what:
                if len(src.shape) == 3:
                    src = src.rearrange("p a b -> p (a b)")
                elif len(src.shape) == 4:
                    src = src.rearrange("p a b c -> p (a b c)")
                n = src.shape[1]
                landed[phase].append(load(sp, landing.ap[:, at:at + n], src))

        def land(phase):
            if phase not in landed:
                prefetch(phase)
            return landed[phase]

        def settle():
            marks = [(q.sem, q.count) for q in (pe, act, dve, pool)]
            for q in (sp, pe, act, dve, pool):
                q.wait(*marks)

        stores = []

        def layer0_attention():
            H, G, HD = 16, 4, 128
            REP = H // G
            scale = float(HD) ** -0.5
            with ExitStack() as sc:
                def A(*a, **k):
                    return alloc(sc, *a, **k)
                stage = Ring([Buf(A(f"a_stage{i}", [P, 2048])) for i in range(3)])
                xT = A("a_xT", [P, DC, BATCH * SEQ])
                wkv = [A(f"a_wkv_{s}", [P, DC, 2 * G * HD], F32R) for s in ("hi", "lo")]
                wq = [A(f"a_wq_{s}", [P, G, DC, REP * HD], F32R) for s in ("hi", "lo")]
                wo = [A(f"a_wo_{s}", [P, H, D], F32R) for s in ("hi", "lo")]
                rope = A("a_rope", [P, 2, SEQ])
                kT = [Ring([Buf(A(f"a_kT{i}_{s}", [P, G, SEQ], F32R)) for i in range(2)]) for s in ("hi", "lo")]
                V = Ring([Buf(A(f"a_V{i}", [P, 2, G * HD])) for i in range(2)])
                qT = Ring([Buf([A(f"a_qT{i}_{s}", [P, 2, SEQ], F32R) for s in ("hi", "lo")]) for i in range(4)])
                t1 = Ring([Buf(A(f"a_t1_{i}", [P, 2, SEQ])) for i in range(2)])
                t2 = Ring([Buf(A(f"a_t2_{i}", [P, 2, SEQ])) for i in range(2)])
                Pm = Ring([Buf(A(f"a_P{i}", [P, 384])) for i in range(3)])
                PT = Ring([Buf(A(f"a_PT{i}", [P, 384])) for i in range(2)])
                OT = Ring([Buf([A(f"a_OT{i}_{s}", [P, SEQ], F32R) for s in ("hi", "lo")]) for i in range(2)])
                st = Ring([Buf(A(f"a_st{i}", [P, 8])) for i in range(4)])

                xT_dram = t["xT"].rearrange("(c p) n -> p c n", p=P)
                kv_stage = stage.next()
                kv_in = kv_stage.ap[:].rearrange("p (c n) -> p c n", c=DC)
                m_xT = [load(sp, xT[:, :, tok(0)], xT_dram[:, :, tok(0)])]
                half = G * HD
                m_wkv = [load(act if i else sp, kv_in[:, :, i * half:(i + 1) * half],
                              t["a_wkv"].rearrange("p (c n) -> p c n", c=DC)[:, :, i * half:(i + 1) * half])
                         for i in range(2)]
                m_rope = load(sp, rope[:], t["rope0"])
                mask_f = alloc(sc, "mask_f", [P, 448])
                load_constants(mask_f)
                wq_stage = [stage.next() for _ in range(2)]
                m_wq = [load(sp, s.ap[:], t["a_wq"][i]) for i, s in enumerate(wq_stage)]
                m_xT.append(load(act, xT[:, :, SEQ:], xT_dram[:, :, SEQ:]))
                x_loaded.append(load(act, X[:], t["x"].rearrange("(n p) d -> p n d", p=P)))

                def split_xt(b, on):
                    xt_ready[b] = split(xT[:, :, tok(b)], XT_hi[:, :, tok(b)], XT_lo[:, :, tok(b)],
                                        [m_xT[min(b, 1)]], lo_on=on)

                split_xt(0, dve)
                kv_ready = []
                for i in range(2):
                    cols = slice(i * half, (i + 1) * half)
                    kv_ready.append(split(kv_in[:, :, cols], wkv[0][:, :, cols], wkv[1][:, :, cols],
                                          [m_wkv[i]], lo_on=dve))
                kv_stage.free = kv_ready[0] + kv_ready[1]
                dve.wait(ready_c)
                m_masks = [dve.put(nc.vector.tensor_copy(ident_b[:], ident[:])),
                           dve.put(nc.vector.tensor_copy(mask_b[:], mask_f[:]))]
                pe.wait(m_masks)
                wq_ready = []

                def split_wq(g, on):
                    s = wq_stage[g // 2]
                    v = s.ap[:].rearrange("p (g c n) -> p g c n", g=2, c=DC)
                    wq_ready.append(split(v[:, g % 2], wq[0][:, g], wq[1][:, g], [m_wq[g // 2]], lo_on=on))
                    s.free = wq_ready[-1] + wq_ready[-1 - g % 2]

                split_wq(0, dve)
                wo_ready = []

                def split_wo():
                    for h4 in range(4):
                        if h4 % 2 == 0:
                            s = stage.next()
                            sp.wait(*s.free)
                            m = load(sp, s.ap[:], t["a_wo"][h4 // 2])
                            v = s.ap[:].rearrange("p (h n) -> p h n", n=D)
                            free = []
                            yield
                        at = slice(4 * (h4 % 2), 4 * (h4 % 2) + 4)
                        wo_ready.append(split(v[:, at], wo[0][:, 4 * h4:4 * h4 + 4], wo[1][:, 4 * h4:4 * h4 + 4],
                                              [m], lo_on=dve if h4 == 0 else pool))
                        free += wo_ready[-1]
                        s.free = free
                        yield

                for p_ in Pm.bufs:
                    p_.free = [pool.put(nc.gpsimd.memset(p_.ap[:, 128:192], 0.0))]

                proj = Ring(psum[0:2])
                score = Ring(psum[2:4])
                pt_bank = Ring(psum[4:5])
                o_bank = Ring(psum[5:6])
                acc_bank = Ring(psum[6:7])
                misc = psum[7]

                def rotate(bank, m, hi, lo, free):
                    src = bank.ap[:, :].rearrange("p (h n) -> p h n", h=2)
                    a, b_ = t1.next(), t2.next()
                    dve.wait(m, m_rope, *a.free, *b_.free)
                    cos = rope[:, 0:1, :].broadcast_to([P, 2, SEQ])
                    ms = [dve.put(nc.vector.tensor_tensor(a.ap[:], src, cos, ALU.mult))]
                    for o, i in ((0, 64), (64, 0)):
                        sin = rope[i:i + 64, 1:2, :].broadcast_to([64, 2, SEQ])
                        ms.append(dve.put(nc.vector.tensor_tensor(b_.ap[o:o + 64], src[i:i + 64], sin, ALU.mult)))
                    bank.free = ms
                    pool.wait(*ms)
                    m = pool.put(nc.gpsimd.tensor_tensor(a.ap[:], a.ap[:], b_.ap[:], ALU.add))
                    b_.free = [m]

                    def halves():
                        a.free = split(a.ap[:], hi, lo, [m], free)
                        return a.free
                    return halves

                class Batch:
                    pass

                bt = {}

                def kv_project(b):
                    s = bt[b] = Batch()
                    s.k = [r.next() for r in kT]
                    s.v = V.next()
                    s.k_ready = []
                    for gp in range(G // 2):
                        bank = proj.next()
                        pe.wait(*kv_ready[0], *xt_ready[b], *bank.free)
                        for j in range(2):
                            g = 2 * gp + j
                            for c in range(DC):
                                w = [x[:, c, g * HD:(g + 1) * HD] for x in wkv]
                                last = mm3(bank.ap[:, j * SEQ:(j + 1) * SEQ], w,
                                           (XT_hi[:, c, tok(b)], XT_lo[:, c, tok(b)]), c == 0, c == DC - 1)
                        m = pe.put(last)
                        halves = rotate(bank, m, s.k[0].ap[:, 2 * gp:2 * gp + 2, :],
                                        s.k[1].ap[:, 2 * gp:2 * gp + 2, :], s.k[0].free)
                        yield
                        s.k_ready += halves()
                        yield
                    ms = []
                    for i in range(2):
                        bank = proj.next()
                        pe.wait(*kv_ready[1], *bank.free)
                        cols = slice(b * SEQ + i * P, b * SEQ + (i + 1) * P)
                        for c in range(DC):
                            last = mm3(bank.ap[:, :], (XT_hi[:, c, cols], XT_lo[:, c, cols]),
                                       [x[:, c, G * HD:] for x in wkv], c == 0, c == DC - 1)
                        m = pe.put(last)
                        act.wait(m, *s.v.free)
                        m = act.put(nc.scalar.copy(s.v.ap[:, i, :], bank.ap[:, :]))
                        bank.free = [m]
                        ms.append(m)
                        yield
                    s.v_ready = ms

                def q_project(b, hp):
                    g, j0 = hp // 2, (hp % 2) * 2
                    bank = proj.next()
                    q = qT.next()
                    pe.wait(*wq_ready[g], *xt_ready[b], *bank.free)
                    for j in range(2):
                        for c in range(DC):
                            w = [x[:, g, c, (j0 + j) * HD:(j0 + j + 1) * HD] for x in wq]
                            last = mm3(bank.ap[:, j * SEQ:(j + 1) * SEQ], w,
                                       (XT_hi[:, c, tok(b)], XT_lo[:, c, tok(b)]), c == 0, c == DC - 1)
                    m = pe.put(last)
                    if hp == H // 2 - 1:
                        xt_read[b].append(m)
                    q.rotate = lambda: rotate(bank, m, q.ap[0][:], q.ap[1][:], q.free)
                    return q

                def scores(b, h, q):
                    s = bt[b]
                    g, j = h // REP, h % 2
                    bank = score.next()
                    pe.wait(*s.k_ready, *q.ready, *bank.free)
                    kh, kl = s.k[0].ap[:, g, :], s.k[1].ap[:, g, :]
                    for i in range(2):
                        o = bank.ap[:, i * SEQ:(i + 1) * SEQ]
                        rows = slice(i * P, (i + 1) * P)
                        mm3(o, (q.ap[0][:, j, rows], q.ap[1][:, j, rows]), (kh, kl), True, False)
                        if i == 0:
                            last = mm(bank.ap[:, 0:128], ident_b[:], window0, False, True)
                        else:
                            last = mm(bank.ap[:, 320:512], ident_b[:], window1, False, True)
                    m = pe.put(last)
                    if j == 1:
                        q.free = [m]
                    S = st.next()
                    p_ = Pm.next()
                    dve.wait(m, *S.free)
                    views = (bank.ap[:, 0:128], bank.ap[:, 320:512])
                    outs = (p_.ap[:, 0:128], p_.ap[:, 192:384])
                    ms = [dve.put(nc.vector.tensor_reduce(S.ap[:, i:i + 1], views[i], AX.X, ALU.max, negate=True))
                          for i in range(2)]
                    dve.wait(*ms)
                    m = dve.put(nc.vector.tensor_scalar(S.ap[:, 2:4], S.ap[:, 0:2], scale, None, ALU.mult))
                    return m, S, p_, bank, views, outs

                def exponentials(got):
                    m, S, p_, bank, views, outs = got
                    act.wait(m, *p_.free)
                    ms = [act.put(nc.scalar.activation(outs[i], views[i], ACT.Exp, bias=S.ap[:, 2 + i:3 + i],
                                                       scale=scale, accum_out=S.ap[:, 4 + i:5 + i]))
                          for i in range(2)]
                    bank.free = p_.exp = ms
                    p_.S, p_.outs = S, outs
                    return p_

                def normalise(p_):
                    S, outs = p_.S, p_.outs
                    dve.wait(*p_.exp)
                    m = dve.put(nc.vector.reciprocal(S.ap[:, 6:8], S.ap[:, 4:6]))
                    dve.wait(m)
                    p_.ready = [dve.put(nc.vector.tensor_scalar(outs[i], outs[i], S.ap[:, 6 + i:7 + i], None,
                                                                ALU.mult)) for i in range(2)]
                    S.free = p_.ready

                def turn(b, h, p_):
                    bank = pt_bank.next()
                    pe.wait(*p_.ready, *bank.free)
                    for i in range(3):
                        last = nc.tensor.transpose(bank.ap[:, i * P:(i + 1) * P], p_.ap[:, i * P:(i + 1) * P], ident[:])
                    m = pe.put(last)
                    p_.free = [m]
                    x = PT.next()
                    act.wait(m, *x.free)
                    m = act.put(nc.scalar.copy(x.ap[:], bank.ap[:, 0:384]))
                    bank.free = [m]
                    x.ready = [m]
                    return x

                def values(b, h, x):
                    s, g = bt[b], h // REP
                    bank = o_bank.next()
                    pe.wait(*x.ready, *s.v_ready, *bank.free)
                    mm(bank.ap[:, 0:256], s.v.ap[:, 0, g * HD:(g + 1) * HD], x.ap[:, 0:256], True, False)
                    m = pe.put(mm(bank.ap[:, 128:256], s.v.ap[:, 1, g * HD:(g + 1) * HD], x.ap[:, 256:384], False, True))
                    x.free = [m]
                    if h == H - 1:
                        s.v.free = [m]
                        s.k[0].free = s.k[1].free = [m]
                    o = OT.next()
                    o.ready = split(bank.ap[:, 0:256], o.ap[0][:], o.ap[1][:], [m], o.free, lo_on=dve)
                    bank.free = o.ready
                    return o

                def project_out(b, h, o):
                    s = bt[b]
                    if h == 0:
                        s.acc = acc_bank.next()
                        pe.wait(*s.acc.free)
                    pe.wait(*o.ready, *wo_ready[h // 4])
                    for i in range(2):
                        rows = slice(i * P, (i + 1) * P)
                        last = mm3(s.acc.ap[:, i * D:(i + 1) * D], (o.ap[0][:, rows], o.ap[1][:, rows]),
                                   [w[:, h, :] for w in wo], h == 0 and i == 0, h == H - 1)
                    o.free = [pe.put(last)]

                def finish(b):
                    s = bt[b]
                    dve.wait(*pe_mark(), *x_ready[b])
                    v = s.acc.ap[:, :].rearrange("p (t n) -> p t n", t=2)
                    m = dve.put(nc.vector.tensor_tensor(X[:, 2 * b:2 * b + 2, :], v, X[:, 2 * b:2 * b + 2, :], ALU.add))
                    s.acc.free = [m]
                    yield
                    yield from norm_out_many(b, [m], misc)

                def pe_mark():
                    return [(pe.sem, pe.count)]

                N = BATCH * H
                qs, ps, xs, os_ = {}, {}, {}, {}
                for _ in kv_project(0):
                    pass
                for k in range(2):
                    qs[k] = q_project(0, k)
                    qs[k].ready = qs[k].rotate()()
                weights = split_wo()
                advance(weights, 2)
                side = None
                tail = None
                for i in range(N + 3):
                    b, h = divmod(i, H)
                    if i < 3:
                        split_wq(i + 1, pool)
                        split_xt(i + 1, pool)
                    else:
                        advance(weights)
                    if i >= 1 and i - 1 < N:
                        normalise(ps[i - 1])
                    if i < N:
                        if h == 0 and side is not None:
                            for _ in side:
                                pass
                        raw = scores(b, h, qs[i // 2])
                        if i % 2 == 1 and i + 3 < N:
                            late = qs[i // 2 + 2]
                            late.halves = late.rotate()
                    if 0 <= i - 2 < N:
                        os_[i - 2] = values(*divmod(i - 2, H), xs[i - 2])
                    advance(tail)
                    if 0 <= i - 3 < N:
                        project_out(*divmod(i - 3, H), os_[i - 3])
                        if (i - 3) % H == H - 1:
                            for _ in tail or ():
                                pass
                            tail = finish((i - 3) // H)
                            advance(tail)
                    if i < N:
                        ps[i] = exponentials(raw)
                    if 0 <= i - 1 < N:
                        xs[i - 1] = turn(*divmod(i - 1, H), ps[i - 1])
                    if i % 2 == 0 and i >= 2 and i + 2 < N:
                        k = i // 2 + 1
                        qs[k].ready = qs[k].halves()
                    if i % 2 == 0 and i + 4 < N:
                        b2, h2 = divmod(i + 4, H)
                        k = i // 2 + 2
                        qs[k] = q_project(b2, h2 // 2)
                    if h == 4 and b + 1 < BATCH:
                        side = kv_project(b + 1)
                    if h >= 4 and i % 2 == 1:
                        advance(side)
                carried[BATCH - 1] = tail

        def narrow_attention(name, hd, heads, kv_heads, weights, k_contraction, q_sign, k_sign,
                             expand, source, out_of, following):
            scale = float(hd) ** -0.5
            T = P // (4 * hd)
            U = heads // T
            PAIRS = T // 2
            per_out = P // hd
            rep = heads // kv_heads
            gap = P - hd
            kc = t[weights[1]].shape[1]
            kvw = kv_heads * hd
            with ExitStack() as sc:
                def A(n, *a, **k):
                    return alloc(sc, f"{name}_{n}", *a, **k)

                def weight(n, key, chunks, width, pieces, in_landing=None):
                    w = [A(f"{n}_{x}", [P, chunks, width], F32R) for x in ("hi", "lo")]
                    if in_landing is None:
                        s = A(n + "_stage", [P, chunks, width])
                        m = load(sp, s[:], t[key])
                    else:
                        m, at = in_landing
                        s = landing.ap[:, at:at + chunks * width].rearrange("p (c n) -> p c n", c=chunks)
                    step = width // pieces

                    def piece(i, on):
                        cols = slice(i * step, (i + 1) * step)
                        return split(s[:, :, cols], w[0][:, :, cols], w[1][:, :, cols], [m], lo_on=on)
                    return w, piece

                m_wq, m_wk = land(name)
                PIECES = U // 2
                wq, wq_piece = weight("wq", weights[0], DC, heads * 4 * hd, PIECES, (m_wq, 0))
                wk, wk_piece = weight("wk", weights[1], kc, heads * 4 * hd, PIECES, (m_wk, 2048))
                wv, wv_piece = weight("wv", weights[2], kc, kvw, 1)
                wo, wo_piece = weight("wo", weights[3], DC, D, 1)
                ex = A("expand", [heads, 2, P])
                ex_ready = load(sp, ex[:], t[expand])

                V = Ring([Buf(A(f"V{i}", [P, 2, kv_heads, P + gap])) for i in range(2)])
                kbd = Ring([Buf(A(f"kbd{i}", [P, T, SEQ], F32R)) for i in range(2)])

                def clear_values(v):
                    v.free = [pool.put(nc.gpsimd.memset(v.ap[:], 0.0))]

                clear_values(V.bufs[0])
                def clear_keys(v):
                    v.free = [dve.put(nc.vector.memset(v.ap[:].bitcast(F32), 0.0))]

                clear_keys(kbd.bufs[0])
                wqk_ready = [wq_piece(0, dve) + wk_piece(0, dve)]
                clear_keys(kbd.bufs[1])
                wv_ready = wv_piece(0, pool)

                def later_weights():
                    for i in range(1, PIECES):
                        wqk_ready.append(wq_piece(i, pool) + wk_piece(i, pool))
                        yield
                        if i == 2:
                            clear_values(V.bufs[1])
                    landing.free = [m for ms in wqk_ready for m in ms]
                    wo_ready.extend(wo_piece(0, pool))
                    yield
                    prefetch(following)

                wo_ready = []
                qpack = Ring([Buf(A(f"qpack{i}", [P, SEQ], F32R)) for i in range(2)])
                parts = Ring([Buf(A(f"parts{i}", [P, 512], F32R)) for i in range(2)])
                P0 = Ring([Buf(A(f"P0_{i}", [P, T, P])) for i in range(2)])
                P1 = Ring([Buf(A(f"P1_{i}", [P, T, SEQ])) for i in range(2)])
                PT = Ring([Buf(A(f"PT{i}", [P, 384])) for i in range(2 * T)])
                st = Ring([Buf(A(f"st{i}", [P, 4 * T])) for i in range(3)])
                sums = Ring([Buf(A(f"sums{i}", [P, 2, heads])) for i in range(2)])
                rT = Ring([Buf(A(f"rT{i}", [heads, SEQ])) for i in range(2)])
                R = Ring([Buf(A(f"R{i}", [P, SEQ])) for i in range(2)])
                OT = Ring([Buf([A(f"OT{i}_{x}", [P, 2, SEQ], F32R) for x in ("hi", "lo")]) for i in range(2)])

                heads_out = Ring([Buf(A(f"heads_out{i}", [P, 1, SEQ])) for i in range(4)])
                proj = Ring(psum[0:1] + psum[3:4] if PAIRS == 1 else psum[0:1])
                S0 = Ring(psum[1:2])
                S1 = Ring(psum[2:2 + PAIRS])
                pt_bank = Ring(psum[4:6])
                o_bank = Ring(psum[6:7])
                misc = psum[7]

                class Batch:
                    pass

                bt = {}

                def value_project(b):
                    finish_carried(b)
                    s = bt[b]
                    marks, parts_of = k_contraction(b)
                    for i in range(2):
                        pe.wait(*wv_ready, *marks, *misc.free)
                        n = 0
                        prods = [(l, r) for c in range(kc) for l, r in parts_of(c, i, [w[:, c, :] for w in wv])]
                        for n, (l, r) in enumerate(prods):
                            last = mm(misc.ap[:, 0:kvw], l, r, n == 0, n == len(prods) - 1)
                        m = pe.put(last)
                        act.wait(m, *s.v.free)
                        m = act.put(nc.scalar.copy(s.v.ap[:, i, :, gap:gap + hd],
                                                   misc.ap[:, 0:kvw].rearrange("p (h d) -> p h d", d=hd)))
                        misc.free = [m]
                        s.v_ready.append(m)
                        yield

                def qk_project(b, u):
                    finish_carried(b)
                    bank, h_, q, k = proj.next(), parts.next(), qpack.next(), kbd.next()
                    cols = slice(u * P, (u + 1) * P)
                    src_hi, src_lo = source
                    pe.wait(*wqk_ready[u // 2], *xt_ready[b], *bank.free)
                    for c in range(DC):
                        mm3(bank.ap[:, 0:SEQ], [w[:, c, cols] for w in wq],
                            (src_hi[:, c, tok(b)], src_lo[:, c, tok(b)]), c == 0, c == DC - 1)
                    marks, parts_of = k_contraction(b)
                    pe.wait(*marks)
                    prods = [(l, r) for c in range(kc) for r, l in parts_of(c, None, [w[:, c, cols] for w in wk])]
                    for n, (l, r) in enumerate(prods):
                        last = mm(bank.ap[:, SEQ:], l, r, n == 0, n == len(prods) - 1)
                    m = pe.put(last)
                    if u == U - 1:
                        xt_read[b].append(m)
                    act.wait(m, *h_.free)
                    m1 = act.put(nc.scalar.copy(h_.ap[:], bank.ap[:, :]))
                    return q, k, h_, bank, m1

                def pack(got):
                    q, k, h_, bank, m1 = got
                    dve.wait(m1, *q.free, *k.free)
                    hv = h_.ap[:].bitcast(F32)
                    q.ready = [dve.put(nc.vector.scalar_tensor_tensor(
                        q.ap[:], hv[:, 0:SEQ], signs[:, q_sign:q_sign + 1], bank.ap[:, 0:SEQ], ALU.mult, ALU.add))]
                    k.ready = []
                    R_ = P // T
                    for j in range(T):
                        rows = slice(j * R_, (j + 1) * R_)
                        k.ready.append(dve.put(nc.vector.scalar_tensor_tensor(
                            k.ap[rows, j, :], hv[rows, SEQ:], signs[rows, k_sign:k_sign + 1],
                            bank.ap[rows, SEQ:], ALU.mult, ALU.add)))
                    h_.free = bank.free = q.ready + k.ready

                def scores(b, u, qk):
                    q, k = qk[0:2]
                    p0, p1, S = P0.next(), P1.next(), st.next()
                    p0.ready, p1.ready = [], []
                    bank0 = S0.next()
                    pe.wait(*q.ready, *k.ready, *bank0.free)
                    w0 = T * P
                    v0 = bank0.ap[:, 0:w0].rearrange("p (h n) -> p h n", h=T)
                    mm(v0, q.ap[:, 0:P], k.ap[:, :, 0:P], True, False)
                    for j in range(T):
                        last = mm(v0[:, j, :], ident_b[:], causal, False, j == T - 1)
                    m = pe.put(last)
                    dve.wait(m, *S.free)
                    m0 = dve.put(nc.vector.tensor_reduce(S.ap[:, 0:T], v0, AX.X, ALU.max, negate=True))
                    dve.wait(m0)
                    m0 = dve.put(nc.vector.tensor_scalar(S.ap[:, 2 * T:3 * T], S.ap[:, 0:T], scale, None, ALU.mult))
                    views = []
                    ms = []
                    for pr in range(PAIRS):
                        bank = S1.next()
                        pe.wait(*bank.free)
                        v = bank.ap[:, :].rearrange("p (h n) -> p h n", h=2)
                        mm(bank.ap[:, :], q.ap[:, P:SEQ], k.ap[:, 2 * pr:2 * pr + 2, :], True, False)
                        for j in range(2):
                            last = mm(v[:, j, P:SEQ], ident_b[:], causal, False, j == 1)
                        m = pe.put(last)
                        dve.wait(m)
                        ms.append(dve.put(nc.vector.tensor_reduce(S.ap[:, T + 2 * pr:T + 2 * pr + 2], v, AX.X,
                                                                  ALU.max, negate=True)))
                        views.append((bank, v))
                    q.free = k.free = [m]
                    dve.wait(*ms)
                    m1 = dve.put(nc.vector.tensor_scalar(S.ap[:, 3 * T:4 * T], S.ap[:, T:2 * T], scale, None, ALU.mult))
                    return (m0, m1), p0, p1, S, bank0, v0, views

                def exponentials(b, u, got):
                    (m0, m1), p0, p1, S, bank0, v0, views = got
                    s = bt[b]
                    act.wait(m0, *p0.free, *p1.free, *s.sums.free)
                    for j in range(T):
                        p0.ready.append(act.put(nc.scalar.activation(
                            p0.ap[:, j, :], v0[:, j, :], ACT.Exp, bias=S.ap[:, 2 * T + j:2 * T + j + 1],
                            scale=scale, accum_out=s.sums.ap[:, 0, u * T + j:u * T + j + 1])))
                    bank0.free = [p0.ready[-1]]
                    act.wait(m1)
                    for j in range(T):
                        bank, v = views[j // 2]
                        p1.ready.append(act.put(nc.scalar.activation(
                            p1.ap[:, j, :], v[:, j % 2, :], ACT.Exp, bias=S.ap[:, 3 * T + j:3 * T + j + 1],
                            scale=scale, accum_out=s.sums.ap[:, 1, u * T + j:u * T + j + 1])))
                        bank.free = [p1.ready[-1]]
                    S.free = [p1.ready[-1]]
                    s.sums_ready = [p0.ready[-1], p1.ready[-1]]
                    return p0, p1

                def turn(u, j, ps):
                    p0, p1 = ps
                    bank, x = pt_bank.next(), PT.next()
                    pe.wait(p0.ready[j], p1.ready[j], *bank.free)
                    for n, src in enumerate((p0.ap[:, j, :], p1.ap[:, j, 0:P], p1.ap[:, j, P:SEQ])):
                        last = nc.tensor.transpose(bank.ap[:, n * P:(n + 1) * P], src, ident[:])
                    m = pe.put(last)
                    if j == T - 1:
                        p0.free = p1.free = [m]
                    eng = dve if j == 1 else act
                    eng.wait(m, *x.free)
                    if eng is act:
                        m = act.put(nc.scalar.copy(x.ap[:], bank.ap[:, 0:384]))
                    else:
                        m = dve.put(nc.vector.tensor_copy(x.ap[:], bank.ap[:, 0:384]))
                    bank.free = x.ready = [m]
                    return x

                def values(b, h, x):
                    s = bt[b]
                    at = h % per_out
                    if at == 0:
                        s.o = o_bank.next()
                        pe.wait(*s.o.free)
                    lo_ = gap - at * hd
                    w = [s.v.ap[:, i, h // rep, lo_:lo_ + P] for i in range(2)]
                    pe.wait(*x.ready, *s.v_ready)
                    mm(s.o.ap[:, 0:SEQ], w[0], x.ap[:, 0:SEQ], at == 0, False)
                    m = pe.put(mm(s.o.ap[:, P:SEQ], w[1], x.ap[:, SEQ:384], False, at == per_out - 1))
                    x.free = [m]
                    if h == heads - 1:
                        s.v.free = [m]
                    if at == per_out - 1:
                        g = h // per_out
                        o32 = heads_out.next()
                        s.o32 = [o32] if g == 0 else s.o32 + [o32]
                        dve.wait(m, *o32.free)
                        r = dve.put(nc.vector.tensor_copy(o32.ap[:, 0, :], s.o.ap[:, 0:SEQ]))
                        s.o.free = [r]
                        s.O_ready.append(r)

                STEPS_TO_NORM = 7

                def finish(b):
                    s = bt[b]
                    dve.wait(*s.sums_ready)
                    m = dve.put(nc.vector.reciprocal(s.sums.ap[:], s.sums.ap[:]))
                    yield
                    pe.wait(m, *misc.free)
                    for i in range(2):
                        last = nc.tensor.transpose(misc.ap[0:heads, i * P:(i + 1) * P], s.sums.ap[:, i, :], ident[:])
                    m = pe.put(last)
                    s.sums.free = [m]
                    yield
                    act.wait(m, *s.rT.free)
                    m = act.put(nc.scalar.copy(s.rT.ap[:], misc.ap[0:heads, 0:SEQ]))
                    misc.free = [m]
                    yield
                    ready = []
                    for g in range(2):
                        r = R.next()
                        pe.wait(m, ex_ready, *misc.free)
                        mr = pe.put(mm(misc.ap[:, 0:SEQ], ex[:, g, :], s.rT.ap[:], True, True))
                        if g == 1:
                            s.rT.free = [mr]
                        yield
                        act.wait(mr, *r.free)
                        mc = act.put(nc.scalar.copy(r.ap[:], misc.ap[:, 0:SEQ]))
                        misc.free = [mc]
                        o = s.o32[g].ap[:, 0, :]
                        pool.wait(mc, s.O_ready[g])
                        m2 = pool.put(nc.gpsimd.tensor_tensor(o, o, r.ap[:], ALU.mult))
                        r.free = [m2]
                        ms = split(o, s.OT.ap[0][:, g, :], s.OT.ap[1][:, g, :], [m2], s.OT.free)
                        s.o32[g].free = ms
                        ready += ms
                        yield
                    pe.wait(*ready, *wo_ready, *misc.free)
                    for i in range(2):
                        rows = slice(i * P, (i + 1) * P)
                        for c in range(DC):
                            last = mm3(misc.ap[:, i * D:(i + 1) * D], (s.OT.ap[0][:, c, rows], s.OT.ap[1][:, c, rows]),
                                       [w[:, c, :] for w in wo], i == 0 and c == 0, c == DC - 1)
                    m = pe.put(last)
                    s.OT.free = [m]
                    dve.wait(m, *x_ready[b])
                    v = misc.ap[:, :].rearrange("p (t n) -> p t n", t=2)
                    m = dve.put(nc.vector.tensor_tensor(X[:, 2 * b:2 * b + 2, :], v, X[:, 2 * b:2 * b + 2, :], ALU.add))
                    misc.free = [m]
                    x_ready[b] = [m]
                    yield
                    for _ in out_of(b, m, misc):
                        yield

                N = BATCH * U
                def start(b):
                    s = bt[b] = Batch()
                    s.v, s.sums, s.rT, s.OT = V.next(), sums.next(), rT.next(), OT.next()
                    s.v_ready, s.O_ready = [], []

                start(0)
                vp = value_project(0)
                qk, pp = {0: qk_project(0, 0)}, {}
                pack(qk[0])
                side = tail = None
                more = later_weights()
                for i in range(N + 1):
                    b, u = divmod(i, U)
                    if i + 1 < N:
                        b2, u2 = divmod(i + 1, U)
                        if u2 == 0 and side is not None:
                            for _ in side:
                                pass
                        if u2 % 2 == 1:
                            advance(more)
                        advance_carried()
                        qk[i + 1] = qk_project(b2, u2)
                    xs = []
                    bp, up = divmod(i - 1, U)
                    if i >= 1:
                        xs += [turn(up, j, pp[i - 1]) for j in range(2)]
                    if i < N:
                        raw = scores(b, u, qk[i])
                    if i >= 1:
                        xs += [turn(up, j, pp[i - 1]) for j in range(2, T)]
                    if i + 1 < N:
                        pack(qk[i + 1])
                    if i < N:
                        exponentials(b, u, raw)
                        pp[i] = raw[1:3]
                    if i == 0:
                        for _ in vp:
                            pass
                    advance(tail)
                    if u == U - 4 and b + 1 < BATCH:
                        start(b + 1)
                        side = value_project(b + 1)
                    if i >= 1:
                        for j in range(T):
                            values(bp, up * T + j, xs[j])
                            if j == 0 and u >= U - 4:
                                advance(side)
                        advance(tail)
                        if up == U - 1:
                            for _ in tail or ():
                                pass
                            tail = finish(bp)
                            advance(tail)
                for _ in range(STEPS_TO_NORM):
                    advance(tail)
                carried[BATCH - 1] = tail

        def norm_out(b, m, bank):
            yield
            yield from norm_out_many(b, [m], bank)

        def from_xt(b):
            def parts_of(c, i, w):
                cols = tok(b) if i is None else slice(b * SEQ + i * P, b * SEQ + (i + 1) * P)
                hi, lo = XT_hi[:, c, cols], XT_lo[:, c, cols]
                return [(hi, w[0]), (hi, w[1]), (lo, w[0])]
            return xt_ready[b] or [], parts_of

        def cross_attention_0():
            with ExitStack() as sc:
                stage = alloc(sc, "b_ctx_stage", [P, BATCH * SEQ])
                parts = alloc(sc, "b_ctx", [P, BATCH * SEQ], F32R)
                packed = alloc(sc, "b_ctx_hi", [P, BATCH * SEQ], F32R)
                m = load(act, stage[:], t["ctxT"])
                act.wait(m)
                m = act.put(nc.scalar.copy(packed[:], stage[:]))
                dve.wait(m, *ready_c)
                m = dve.put(nc.vector.scalar_tensor_tensor(parts[:], packed[:].bitcast(F32), signs[:, 4:5], stage[:],
                                                           ALU.mult, ALU.add))

                def contraction(b):
                    def parts_of(c, i, w):
                        cols = tok(b) if i is None else slice(b * SEQ + i * P, b * SEQ + (i + 1) * P)
                        return [(parts[:, cols], w[0]), (parts[:, cols], w[1])]
                    return [m], parts_of

                narrow_attention("b", 16, 16, 16, ("b_wq", "b_wk", "b_wv", "b_wo"), contraction, 0, 1,
                                 "expand16", (XT_hi, XT_lo), norm_out, "c")

        def experts(name, w_dram, gate_dram, capped, out_of, following):
            E, INTER = 8, 512
            IC = INTER // P
            HALF = 2 * SEQ
            with ExitStack() as sc:
                def A(n, *a, **k):
                    return alloc(sc, f"{name}_{n}", *a, **k)

                m_w0, m_gate = land(name)
                gate_stage = landing.ap[:, 3072:3072 + DC * E].rearrange("p (c e) -> p c e", c=DC)
                gate = [A(f"gate_{x}", [P, DC, E], F32R) for x in ("hi", "lo")]
                iota = A("iota", [P, E])
                m_iota = load(act, iota[:], t["iota8"])
                stage = Ring([Buf(A(f"stage{i}", [P, 3 * DC * INTER])) for i in range(2)])
                W = Ring([Buf([A(f"w{i}_{x}", [P, 3 * DC * INTER], F32R) for x in ("hi", "lo")]) for i in range(2)])
                silu = Ring([Buf(A(f"silu{i}", [P, HALF])) for i in range(3)])
                h32 = Ring([Buf(A(f"h32_{i}", [P, HALF])) for i in range(3)])
                hT = Ring([Buf([A(f"hT{i}_{x}", [P, IC, HALF], F32R) for x in ("hi", "lo")]) for i in range(2)])
                logitT = A("logitT", [E, TILES * P])
                logit = A("logit", [P, TILES, E])
                e_ = A("e", [P, TILES, E])
                wts = A("wts", [P, TILES, E])
                red = A("red", [P, 4, TILES])
                top = A("top", [P, TILES, 8])
                idx = A("idx", [P, TILES, 8], U32)
                idxf = A("idxf", [P, TILES, 8])

                gate_banks = Ring(psum[0:2])
                up_banks = Ring(psum[2:4])
                out_banks = Ring(psum[4:7])
                misc = psum[7]

                def prepare(e):
                    w, n = W.next(), DC * INTER
                    if e == 0:
                        s, m = landing, m_w0
                    else:
                        s = stage.next()
                        sp.wait(*s.free)
                        m = load(sp, s.ap[:], t[w_dram][e])
                    w.ready = []
                    for c in range(3):
                        cols = slice(c * n, (c + 1) * n)
                        w.ready.append(split(s.ap[:, cols], w.ap[0][:, cols], w.ap[1][:, cols], [m], w.free,
                                             lo_on=dve if e == 0 and c < 2 else pool))
                    s.free = [m for ms in w.ready for m in ms]
                    return w

                def route():
                    pe.wait(*gate_ready)
                    for half in range(2):
                        bank = gate_banks.next()
                        pe.wait(*bank.free, *(xt_ready[2 * half] or []), *(xt_ready[2 * half + 1] or []))
                        cols = slice(half * HALF, (half + 1) * HALF)
                        for c in range(DC):
                            last = mm3(bank.ap[0:E, :], [g[:, c, :] for g in gate],
                                       (XT_hi[:, c, cols], XT_lo[:, c, cols]), c == 0, c == DC - 1)
                        m = pe.put(last)
                        act.wait(m)
                        m = act.put(nc.scalar.copy(logitT[:, cols], bank.ap[0:E, :]))
                        bank.free = [m]
                    pe.wait(m, *misc.free)
                    for n in range(TILES):
                        last = nc.tensor.transpose(misc.ap[:, n * E:(n + 1) * E], logitT[:, n * P:(n + 1) * P],
                                                   ident[0:E, 0:E])
                    m = pe.put(last)
                    src = misc.ap[:, 0:TILES * E].rearrange("p (n e) -> p n e", e=E)
                    bc = lambda x: x.unsqueeze(2).broadcast_to([P, TILES, E])
                    if capped:
                        act.wait(m)
                        m = act.put(nc.scalar.activation(e_[:], src, ACT.Tanh, scale=1.0 / capped))
                        misc.free = [m]
                        dve.wait(m)
                        m = dve.put(nc.vector.tensor_scalar(logit[:], e_[:], float(capped), None, ALU.mult))
                    else:
                        dve.wait(m)
                        m = dve.put(nc.vector.tensor_copy(logit[:], src))
                        misc.free = [m]
                    dve.wait(m)
                    m = dve.put(nc.vector.tensor_reduce(red[:, 0, :], logit[:], AX.X, ALU.max))
                    dve.wait(m)
                    m = dve.put(nc.vector.tensor_tensor(e_[:], logit[:], bc(red[:, 0, :]), ALU.subtract))
                    act.wait(m)
                    m = act.put(nc.scalar.activation(e_[:], e_[:], ACT.Exp))
                    key = e_ if capped else logit
                    dve.wait(m)
                    if capped:
                        ms = [dve.put(nc.vector.tensor_reduce(red[:, 1, :], e_[:], AX.X, ALU.add))]
                    else:
                        ms = []
                    tops = [dve.put(nc.vector.max(top[:, n, :], key[:, n, :])) for n in range(TILES)]
                    dve.wait(tops[-1])
                    tops = [dve.put(nc.vector.max_index(idx[:, n, :], top[:, n, :], key[:, n, :]))
                            for n in range(TILES)]
                    dve.wait(tops[-1])
                    m = dve.put(nc.vector.tensor_copy(idxf[:], idx[:]))
                    dve.wait(m, m_iota)
                    ms2 = []
                    for n in range(TILES):
                        ms2.append(dve.put(nc.vector.tensor_scalar(wts[:, n, :], iota[:], idxf[:, n, 0:1], None,
                                                                   ALU.is_equal)))
                    dve.wait(ms2[-1])
                    for n in range(TILES):
                        m = dve.put(nc.vector.scalar_tensor_tensor(wts[:, n, :], iota[:], idxf[:, n, 1:2],
                                                                   wts[:, n, :], ALU.is_equal, ALU.add))
                    dve.wait(m)
                    m = dve.put(nc.vector.tensor_tensor(wts[:], wts[:], e_[:], ALU.mult))
                    if not capped:
                        dve.wait(m)
                        ms = [dve.put(nc.vector.tensor_reduce(red[:, 1, :], wts[:], AX.X, ALU.add))]
                    dve.wait(m, *ms)
                    m = dve.put(nc.vector.reciprocal(red[:, 2, :], red[:, 1, :]))
                    dve.wait(m)
                    return dve.put(nc.vector.tensor_tensor(wts[:], wts[:], bc(red[:, 2, :]), ALU.mult))

                def up(e, half, ic, w, h):
                    g, u = gate_banks.next(), up_banks.next()
                    cols = slice(half * HALF, (half + 1) * HALF)
                    pe.wait(*(xt_ready[2 * half] or []), *(xt_ready[2 * half + 1] or []))
                    n = DC * INTER
                    marks = []
                    for k, bank in enumerate((g, u)):
                        pe.wait(*w.ready[k], *bank.free)
                        for c in range(DC):
                            at = k * n + c * INTER + ic * P
                            last = mm3(bank.ap[:, :], [x[:, at:at + P] for x in w.ap],
                                       (XT_hi[:, c, cols], XT_lo[:, c, cols]), c == 0, c == DC - 1)
                        marks.append(pe.put(last))
                    if e == E - 1 and ic == IC - 1:
                        xt_read[2 * half].append(marks[1])
                        xt_read[2 * half + 1].append(marks[1])
                    s, y = silu.next(), h32.next()
                    act.wait(marks[0], *s.free)
                    m = act.put(nc.scalar.activation(s.ap[:], g.ap[:, :], ACT.Silu))
                    g.free = [m]
                    dve.wait(m, marks[1], *y.free)
                    m = dve.put(nc.vector.tensor_tensor(y.ap[:], u.ap[:, :], s.ap[:], ALU.mult))
                    u.free = s.free = [m]
                    y.free = split(y.ap[:], h.ap[0][:, ic, :], h.ap[1][:, ic, :], [m], h.free if ic == 0 else (),
                                   lo_on=dve)
                    h.ready += y.free

                def down(e, half, w, h, wts_ready):
                    n2 = 2 * DC * INTER
                    pe.wait(*h.ready, *w.ready[2])
                    for pair in range(2):
                        bank = out_banks.next()
                        pe.wait(*bank.free)
                        for i in range(2):
                            rows = slice((2 * pair + i) * P, (2 * pair + i + 1) * P)
                            for ic in range(IC):
                                cols = slice(n2 + ic * D, n2 + (ic + 1) * D)
                                last = mm3(bank.ap[:, i * D:(i + 1) * D], (h.ap[0][:, ic, rows], h.ap[1][:, ic, rows]),
                                           [x[:, cols] for x in w.ap], i == 0 and ic == 0, ic == IC - 1)
                        m = pe.put(last)
                        b = 2 * half + pair
                        ms = []
                        for i in range(2):
                            n = 2 * b + i
                            dve.wait(m, wts_ready, *x_ready[b])
                            ms.append(dve.put(nc.vector.scalar_tensor_tensor(
                                X[:, n, :], bank.ap[:, i * D:(i + 1) * D], wts[:, n, e:e + 1], X[:, n, :],
                                ALU.mult, ALU.add)))
                        bank.free = ms
                        x_ready[b] = ms
                        yield b, ms
                    h.free = [m]
                    if half == 1:
                        w.free = [m]

                w = {0: prepare(0)}
                gate_ready = split(gate_stage, gate[0][:], gate[1][:], [m_gate])
                landing.free = landing.readers + gate_ready
                wts_ready = None
                pending = None
                tails = []
                for e in range(E):
                    for half in range(2):
                        h = hT.next()
                        h.ready = []
                        if e == 3 and half == 0 and following is not None:
                            prefetch(following)
                        for b in range(2 * half, 2 * half + 2):
                            finish_carried(b)
                        for ic in range(IC):
                            if e == 0 and half == 0:
                                advance_carried()
                            up(e, half, ic, w[e], h)
                            if pending is not None and ic in (0, 1):
                                got = next(pending, None)
                                if got and e == E - 1 and half == 1:
                                    tails.append(out_of(got[0], got[1], misc))
                                    carried[got[0]] = tails[-1]
                        if pending is not None:
                            for _ in pending:
                                pass
                        if half == 0 and e + 1 < E:
                            w[e + 1] = prepare(e + 1)
                        if wts_ready is None:
                            for b in range(BATCH):
                                finish_carried(b)
                            wts_ready = route()
                        pending = down(e, half, w[e], h, wts_ready)
                for x in tails:
                    advance(x, STEPS_OF_NORM)
                for b, ms in pending:
                    carried[b] = out_of(b, ms, misc)
                    advance(tails[b - 2])

        def norm_out_many(b, ms, bank):
            yield from layer_norm(b, ms)
            to_xt(b, X[:, 2 * b:2 * b + 2, :], x_ready[b], bank)
            yield

        def latent_attention():
            H, QW, HALFQ = 16, 192, 96
            LAG = 3
            PT_BUFS = LAG + 1
            PIECE = 400
            with ExitStack() as sc:
                def A(n, *a, **k):
                    return alloc(sc, f"e_{n}", *a, **k)

                ropeq = A("ropeq", [HALFQ, 4, SEQ])
                m_ropeq = load(act, ropeq[:], t["ropeq"])
                KTb = [A(f"KT{b}", [P, CTX + 1], F32R) for b in range(BATCH)]
                kvb = [A(f"kv{b}", [P, KT, P], F32R) for b in range(BATCH)]
                kt_ready, kv_ready = [], []
                aux = psum[7]
                score = psum[0:4]
                tb = Ring(psum[4:6])
                ctx_bank = psum[6]

                stage = Ring([Buf(A(f"stage{i}", [P, 832])) for i in range(2)])
                stage_r = Ring([Buf(A(f"stage_r{i}", [LAT, 320])) for i in range(2)])
                wq = Ring([Buf([A(f"wq{i}_{x}", [P, DC, QW], F32R) for x in ("hi", "lo")]) for i in range(2)])
                w2 = Ring([Buf([A(f"w2{i}_{x}", [HALFQ, 2, P], F32R) for x in ("hi", "lo")]) for i in range(2)])
                wf = Ring([Buf([A(f"wf{i}_{x}", [P, D], F32R) for x in ("hi", "lo")]) for i in range(2)])
                r0 = Ring([Buf(A(f"r0_{i}", [HALFQ, 2, SEQ])) for i in range(2)])
                r1 = Ring([Buf(A(f"r1_{i}", [HALFQ, 2, SEQ])) for i in range(2)])
                r2 = Ring([Buf(A(f"r2_{i}", [HALFQ, 2, SEQ])) for i in range(2)])
                qr = Ring([Buf([A(f"qr{i}_{x}", [HALFQ, 2, SEQ], F32R) for x in ("hi", "lo")]) for i in range(2)])
                qk = Ring([Buf([A(f"qk{i}_{x}", [P, SEQ], F32R) for x in ("hi", "lo")]) for i in range(2)])
                def prepare(h):
                    s, r = stage.next(), stage_r.next()
                    sp.wait(*s.free, *r.free)
                    m, mr = load(sp, s.ap[:], t["e_w"][h]), load(sp, r.ap[:], t["e_wr"][h])
                    yield
                    q = wq.next()
                    pe.wait(m, *aux.free)
                    for c in range(DC):
                        last = mm(aux.ap[:, c * QW:(c + 1) * QW], s.ap[:, c * P:(c + 1) * P], s.ap[:, D:D + QW],
                                  True, True)
                    m0 = pe.put(last)
                    yield
                    v = aux.ap[:, 0:DC * QW].rearrange("p (c n) -> p c n", c=DC)
                    hw[h] = [q]
                    q.ready = aux.free = split(v, q.ap[0][:], q.ap[1][:], [m0], q.free, lo_on=dve)
                    yield
                    a = w2.next()
                    pe.wait(mr, *aux.free)
                    for c in range(2):
                        last = mm(aux.ap[0:HALFQ, c * P:(c + 1) * P], r.ap[:, c * HALFQ:(c + 1) * HALFQ],
                                  r.ap[:, QW:QW + P], True, True)
                    m1 = pe.put(last)
                    r.free = [m1]
                    yield
                    v = aux.ap[0:HALFQ, 0:2 * P].rearrange("p (c n) -> p c n", c=2)
                    hw[h].append(a)
                    a.ready = aux.free = split(v, a.ap[0][:], a.ap[1][:], [m1], a.free, lo_on=dve)
                    yield
                    f = wf.next()
                    pe.wait(*aux.free)
                    m2 = pe.put(mm(aux.ap[:, 0:D], s.ap[:, 704:832], s.ap[:, 448:704], True, True))
                    yield
                    hw[h].append(f)
                    f.ready = aux.free = split(aux.ap[:, 0:D], f.ap[0][:], f.ap[1][:], [m2], f.free, lo_on=dve)
                    s.free = [m2]
                    yield

                hw = {}

                class Unit:
                    pass

                def queries(u):
                    finish_carried(u.b)
                    q = hw[u.h][0]
                    cols = tok(u.b)
                    pe.wait(*q.ready, *(xt_ready[u.b] or []), *aux.free)
                    for c in range(2):
                        for d in range(DC):
                            last = mm3(aux.ap[0:HALFQ, c * SEQ:(c + 1) * SEQ],
                                       [w[:, d, c * HALFQ:(c + 1) * HALFQ] for w in q.ap],
                                       (XT_hi[:, d, cols], XT_lo[:, d, cols]), d == 0, d == DC - 1)
                    m = pe.put(last)
                    if u.h == H - 1:
                        xt_read[u.b].append(m)
                    if u.b == BATCH - 1:
                        q.free = [m]
                    yield
                    y, x1, x2, z = r0.next(), r1.next(), r2.next(), qr.next()
                    act.wait(m, *y.free)
                    v = y.ap
                    m = act.put(nc.scalar.copy(v[:].rearrange("p c n -> p (c n)"), aux.ap[0:HALFQ, :]))
                    aux.free = [m]
                    pool.wait(m, m_ropeq, *x1.free, *x2.free)
                    ms = [pool.put(nc.gpsimd.tensor_tensor(x1.ap[:], v[:], ropeq[:, 0:2, :], ALU.mult))]
                    for c in range(2):
                        ms.append(pool.put(nc.gpsimd.tensor_tensor(x2.ap[:, c, :], v[:, 1 - c, :],
                                                                   ropeq[:, 2 + c, :], ALU.mult)))
                    y.free = ms
                    pool.wait(*ms)
                    m = pool.put(nc.gpsimd.tensor_tensor(x1.ap[:], x1.ap[:], x2.ap[:], ALU.add))
                    x2.free = [m]
                    u.z, u.z_sum = z, m
                    u.x1 = x1
                    yield
                    z.ready = x1.free = split(x1.ap[:], z.ap[0][:], z.ap[1][:], [m], z.free)
                    yield
                    k, a = qk.next(), hw[u.h][1]
                    pe.wait(*z.ready, *a.ready, *aux.free)
                    for c in range(2):
                        last = mm3(aux.ap[:, 0:SEQ], [w[:, c, :] for w in a.ap],
                                   (z.ap[0][:, c, :], z.ap[1][:, c, :]), c == 0, c == 1)
                    m = pe.put(last)
                    z.free = [m]
                    if u.b == BATCH - 1:
                        a.free = [m]
                    yield
                    k.ready = split(aux.ap[:, 0:SEQ], k.ap[0][:], k.ap[1][:], [m], k.free, lo_on=dve)
                    aux.free = k.ready
                    u.qk = k
                    yield

                N = H * BATCH
                units = []

                def begin(i):
                    u = Unit()
                    u.h, u.b = divmod(i, BATCH)
                    u.neg, u.r_ready, u.got = {}, [], {}
                    units.append(u)
                    u.queries = queries(u)
                    advance(u.queries)

                def first_queries():
                    for _ in prepare(0):
                        yield
                    begin(0)
                    yield
                    for _ in units[0].queries:
                        yield
                    begin(1)
                    yield
                    advance(units[1].queries)
                    yield
                    advance(units[1].queries)

                with ExitStack() as pre:
                    def B(n, *a, **k):
                        return alloc(pre, f"e_{n}", *a, **k)
                    m_ropek, *m_ctx = land("e")
                    n = KT * LAT
                    ropek = landing.ap[:, 0:2 * n].rearrange("p (a k d) -> p a k d", a=2, k=KT)
                    ctx_in = Ring([Buf(landing.ap[:, (2 + i) * n:(3 + i) * n].rearrange("p (k d) -> p k d", k=KT))
                                   for i in range(2)])
                    turned = Ring([Buf(B(f"turned{i}", [P, KT, LAT])) for i in range(2)])
                    kvd = Ring([Buf(B(f"kvd{i}", [P, KT, 2, LAT])) for i in range(2)])
                    part = Ring([Buf(B(f"part{i}", [P, 512], F32R)) for i in range(3)])
                    banks = Ring(psum[0:6])

                    def rope_context(b):
                        x, r, k = ctx_in.next(), turned.next(), kvd.next()
                        if b < 2:
                            m = m_ctx[b]
                        else:
                            sp.wait(*x.free)
                            m = load(sp, x.ap[:], t["ctx"][b])
                        pool.wait(m, m_ropek, *r.free)
                        ms = [pool.put(nc.gpsimd.tensor_tensor(r.ap[:, :, 0:32], x.ap[:, :, 32:64],
                                                               ropek[:, 1, :, 0:32], ALU.mult)),
                              pool.put(nc.gpsimd.tensor_tensor(r.ap[:, :, 32:64], x.ap[:, :, 0:32],
                                                               ropek[:, 1, :, 32:64], ALU.mult))]
                        dve.wait(*ms)
                        m = dve.put(nc.vector.tensor_tensor(x.ap[:], x.ap[:], ropek[:, 0, :, :], ALU.mult))
                        dve.wait(m, *k.free)
                        ms = [dve.put(nc.vector.tensor_tensor(k.ap[:, :, i, :], x.ap[:], r.ap[:], ALU.add))
                              for i in range(2)]
                        x.free = r.free = landing.free = ms
                        k.ready = ms
                        return k

                    k = rope_context(0)
                    warm = first_queries()
                    advance(warm)
                    for b in range(BATCH):
                        after = rope_context(b + 1) if b + 1 < BATCH else None
                        hi, lo = kvb[b][:, :, 0:LAT], kvb[b][:, :, LAT:P]
                        kv_ready.append(split(k.ap[:, :, 0, :], hi, lo, k.ready, lo_on=pool))
                        pe.wait(*k.ready)
                        ready = [act.put(nc.scalar.copy(KTb[b][:, CTX:CTX + 1], signs[:, 7:8]))]
                        for g in range(0, KT, 4):
                            bank, pt = banks.next(), part.next()
                            pe.wait(*bank.free)
                            n = min(4, KT - g)
                            width = min(CTX - g * P, n * P)
                            for i in range(n):
                                rows = min(P, CTX - (g + i) * P)
                                last = nc.tensor.transpose(
                                    bank.ap[:, i * P:i * P + rows],
                                    k.ap[0:rows, g + i, :, :].rearrange("p a d -> p (a d)"), ident[0:rows, 0:rows])
                            mt = pe.put(last)
                            act.wait(mt, *pt.free)
                            m1 = act.put(nc.scalar.copy(pt.ap[:, 0:width], bank.ap[:, 0:width]))
                            dve.wait(m1)
                            m2 = dve.put(nc.vector.scalar_tensor_tensor(
                                KTb[b][:, g * P:g * P + width], pt.ap[:, 0:width].bitcast(F32), signs[:, 4:5],
                                bank.ap[:, 0:width], ALU.mult, ALU.add))
                            bank.free = pt.free = [m2]
                            ready.append(m2)
                            advance(warm)
                        k.free = [mt] + kv_ready[b]
                        kt_ready.append(ready)
                        k = after
                    for _ in warm:
                        pass
                    drained = kt_ready[-1] + kv_ready[-1] + kt_ready[-2] + kv_ready[-2]

                Pm = Ring([Buf(A(f"P{i}", [P, 2, CTX])) for i in range(2)])
                PT = Ring([Buf([A(f"PT{i}_{x}", [P, 2, SEQ], F32R) for x in ("hi", "lo")]) for i in range(PT_BUFS)])
                st = Ring([Buf(A(f"st{i}", [P, 2, 8])) for i in range(4)])
                cx = Ring([Buf([A(f"cx{i}_{x}", [P, SEQ], F32R) for x in ("hi", "lo")]) for i in range(2)])
                sp.wait(*drained)
                act.wait(*drained)
                dve.wait(*drained)
                pool.wait(*drained)

                def score_piece(u, i, j):
                    k = u.qk
                    rows = slice(i * P, (i + 1) * P)
                    pe.wait(*k.ready, *kt_ready[u.b], *score[j].free)
                    for n in range(2):
                        last = mm(score[j].ap[:, 0:PIECE + 2], k.ap[n][:, rows],
                                  KTb[u.b][:, j * PIECE:j * PIECE + PIECE + 2], n == 0, n == 1)
                    m = pe.put(last)
                    if i == 1 and j == 3:
                        k.free = [m]
                    if i == 0 and j == 0:
                        u.st = st.next()
                    s = u.st
                    dve.wait(m, *s.free)
                    if j == 0:
                        u.maxima = []
                    u.maxima.append(dve.put(nc.vector.tensor_reduce(
                        s.ap[:, i, j:j + 1], score[j].ap[:, 0:PIECE + 1], AX.X, ALU.max)))
                    if j == 3:
                        dve.wait(*u.maxima)
                        u.neg[i] = dve.put(nc.vector.tensor_reduce(s.ap[:, i, 4:5], s.ap[:, i, 0:4], AX.X, ALU.max,
                                                                   negate=True))

                def exponential(u, i, j):
                    if i == 0 and j == 0:
                        u.p = Pm.next()
                        u.p.ready = []
                        act.wait(*u.p.free)
                    s, p = u.st, u.p
                    act.wait(u.neg[i])
                    n = PIECE + (j == 3)
                    m = act.put(nc.scalar.activation(
                        p.ap[:, i, j * PIECE:j * PIECE + n], score[j].ap[:, 0:n], ACT.Exp, bias=s.ap[:, i, 4:5],
                        accum_out=s.ap[:, i, j:j + 1]))
                    score[j].free = [m]
                    p.ready.append(m)

                def row_sums(u, i):
                    s = u.st
                    dve.wait(*u.p.ready)
                    m = dve.put(nc.vector.tensor_reduce(s.ap[:, i, 5:6], s.ap[:, i, 0:4], AX.X, ALU.add))
                    dve.wait(m)
                    u.r_ready.append(dve.put(nc.vector.reciprocal(s.ap[:, i, 6:7], s.ap[:, i, 5:6])))

                GROUPS = -(-KT // 2)

                def turn(u, g):
                    bank, x = tb.next(), PT.next()
                    pe.wait(*u.p.ready, *bank.free)
                    n = min(2, KT - 2 * g)
                    rows = min(P, CTX - 2 * g * P)
                    for c in range(n):
                        k0 = (2 * g + c) * P
                        for i in range(2):
                            last = nc.tensor.transpose(bank.ap[0:rows, c * SEQ + i * P:c * SEQ + (i + 1) * P],
                                                       u.p.ap[:, i, k0:k0 + rows], ident[:])
                    m = pe.put(last)
                    if g == GROUPS - 1:
                        u.p.free = [m]
                    v = bank.ap[0:rows, 0:n * SEQ].rearrange("p (c n) -> p c n", c=n)
                    hi, lo = x.ap[0][0:rows, 0:n, :], x.ap[1][0:rows, 0:n, :]
                    act.wait(m, *x.free)
                    m1 = act.put(nc.scalar.copy(hi, v))

                    def lower():
                        dve.wait(m1)
                        x.ready = [m1, dve.put(nc.vector.tensor_tensor(lo, v, hi.bitcast(F32), ALU.subtract))]
                        bank.free = x.ready
                    return x, n, rows, lower

                def attend(u, g, got):
                    x, n, rows, _ = got
                    if g == 0:
                        pe.wait(*ctx_bank.free)
                    pe.wait(*x.ready, *kv_ready[u.b])
                    for c in range(n):
                        w = kvb[u.b][0:rows, 2 * g + c, :]
                        for y in range(2):
                            last = mm(ctx_bank.ap[:, 0:SEQ], w, x.ap[y][0:rows, c, :],
                                      g == 0 and c == 0 and y == 0, g == GROUPS - 1 and c == n - 1 and y == 1)
                    m = pe.put(last)
                    x.free = [m]
                    u.ctx_done = m

                def keep_context(u):
                    c = u.cx = cx.next()
                    c.ready = split(ctx_bank.ap[:, 0:SEQ], c.ap[0][:], c.ap[1][:], [u.ctx_done], c.free, lo_on=dve)
                    ctx_bank.free = c.ready

                def project_out(u):
                    c, f = u.cx, hw[u.h][2]
                    pe.wait(*c.ready, *f.ready, *aux.free)
                    for i in range(2):
                        rows = slice(i * P, (i + 1) * P)
                        last = mm3(aux.ap[:, i * D:(i + 1) * D], (c.ap[0][:, rows], c.ap[1][:, rows]),
                                   [w[:] for w in f.ap], True, True)
                    m = pe.put(last)
                    c.free = [m]
                    if u.b == BATCH - 1:
                        f.free = [m]
                    yield
                    ms = []
                    for i in range(2):
                        n = 2 * u.b + i
                        dve.wait(m, u.r_ready[i], *x_ready[u.b])
                        ms.append(dve.put(nc.vector.scalar_tensor_tensor(
                            X[:, n, :], aux.ap[:, i * D:(i + 1) * D], u.st.ap[:, i, 6:7], X[:, n, :],
                            ALU.mult, ALU.add)))
                    aux.free = u.st.free = ms
                    x_ready[u.b] = ms
                    yield

                def unit(i):
                    return units[i] if 0 <= i < N else None

                for j in range(4):
                    score_piece(units[0], 0, j)
                prep = None
                for i in range(N + 4):
                    u, v, w, nxt = unit(i), unit(i - 1), unit(i - 2), unit(i + 1)
                    if i % BATCH == 0 and i // BATCH + 1 < H:
                        prep = prepare(i // BATCH + 1)
                    for step in range(2 * 4):
                        half, j = divmod(step, 4)
                        if u is not None:
                            exponential(u, half, j)
                        if step == LAG - 1 and w is not None:
                            keep_context(w)
                        if step == 1 and v is not None:
                            row_sums(v, 1)
                        if step == 2 and nxt is not None:
                            advance(nxt.queries)
                        if step == 4 and i + 2 < N:
                            advance(units[i + 2].queries)
                        if step == 0 and unit(i - 3) is not None:
                            done = unit(i - 3)
                            advance(done.out)
                            if done.h == H - 1:
                                carried[done.b] = norm_into_last(done.b, x_ready[done.b], aux)
                        if N - 1 <= i <= N:
                            advance_carried()
                        if step == 0 and i == N // 2:
                            prefetch("f")
                        if (step == 0 and i % BATCH == 0) or (step == 6 and i % BATCH < 3):
                            advance(prep)
                        if v is not None and step < GROUPS:
                            v.got[step] = turn(v, step)
                        at = step - LAG
                        if at < 0 and w is not None and at + 8 < GROUPS:
                            attend(w, at + 8, w.got[at + 8])
                        if at >= 0 and v is not None:
                            attend(v, at, v.got[at])
                        ahead = u if half == 0 else nxt
                        if ahead is not None and u is not None:
                            score_piece(ahead, 1 - half, j)
                        if v is not None and step < GROUPS:
                            v.got[step][3]()
                        if step == 1 and nxt is not None:
                            advance(nxt.queries)
                        if step == 7 and i + 2 < N:
                            advance(units[i + 2].queries)
                        if step == 3 and i + 2 < N:
                            begin(i + 2)
                        if step == 5 and i % BATCH < 3:
                            advance(prep)
                        if step == 5 and u is not None:
                            row_sums(u, 0)
                        if step == 7 and w is not None:
                            w.out = project_out(w)
                            advance(w.out)

        def rms_to_xt(b, marks, bank, weight):
            T = tiny.next()
            m = row_stats(b, T, marks)
            st_ = T.ap[:, 12:16].rearrange("p (t s) -> p t s", s=2)
            v, y, s = T.ap[:, 16:18], T.ap[:, 18:20], T.ap[:, 20:22]
            dve.wait(m)
            m = dve.put(nc.vector.tensor_tensor(s, st_[:, :, 0], st_[:, :, 0], ALU.mult))
            dve.wait(m)
            m = dve.put(nc.vector.scalar_tensor_tensor(v, s, EPS, st_[:, :, 1], ALU.add, ALU.add))
            m = yield from inv_sqrt(v, y, s, [m])
            y32 = normed.next()
            dve.wait(m, *y32.free)
            ms = [dve.put(nc.vector.tensor_scalar(y32.ap[:, i, :], X[:, 2 * b + i, :], T.ap[:, 18 + i:19 + i], None,
                                                  ALU.mult)) for i in range(2)]
            T.free = ms
            yield
            act.wait(m_ln)
            dve.wait(m_ln)
            y32.free = [to_xt(b, y32.ap, ms, bank, weight)]
            yield

        x_in_ready = {}

        def enter_last(b, ms, bank):
            pair = slice(2 * b, 2 * b + 2)
            act.wait(*ms)
            x_in_ready[b] = act.put(nc.scalar.copy(x_in[:, pair, :], X[:, pair, :]))
            for _ in rms_to_xt(b, ms, bank, ln_w[:, 0:DC]):
                yield

        def norm_into_last(b, ms, bank):
            yield from layer_norm(b, ms)
            yield from enter_last(b, x_ready[b], bank)

        def last_block():
            def middle(b, m, bank):
                for _ in rms_to_xt(b, [m], bank, ln_w[:, DC:2 * DC]):
                    yield
                pair = X[:, 2 * b:2 * b + 2, :]
                dve.wait(x_in_ready[b], *x_ready[b])
                x_ready[b] = [dve.put(nc.vector.tensor_tensor(pair, pair, x_in[:, 2 * b:2 * b + 2, :], ALU.add))]
                yield

            narrow_attention("f", 16, 16, 16, ("f_wq", "f_wk", "f_wv", "f_wo"), from_xt, 0, 1, "expand16",
                             (XT_hi, XT_lo), middle, "g")
            settle()
            experts("g", "g_w", "g_gate", None, store_out, None)
            for b in range(BATCH):
                finish_carried(b)

        def store_out(b, ms, bank):
            yield from layer_norm(b, ms)
            sp.wait(*x_ready[b])
            stores.append(load(sp, out.rearrange("(n p) d -> p n d", p=P)[:, 2 * b:2 * b + 2, :],
                               X[:, 2 * b:2 * b + 2, :]))
            yield

        layer0_attention()
        settle()
        landing.ap = alloc(top, "landing", [P, 4096])
        ln_w = vec("ln_w", [P, 2 * DC])
        x_in = vec("x_in", [P, TILES, D])
        normed = Ring([Buf(vec(f"normed{i}", [P, 2, D])) for i in range(BATCH)])
        m_ln = load(sp, ln_w[:], t["f_ln"])
        cross_attention_0()
        settle()
        experts("c", "c_w", "c_gate", 30.0, norm_out_many, "d")
        settle()
        narrow_attention("d", 8, 32, 8, ("d_wq", "d_wk", "d_wv", "d_wo"), from_xt, 2, 3, "expand8",
                         (XT_hi, XT_lo), norm_out, "e")
        settle()
        latent_attention()
        settle()
        last_block()

        sp.wait(*stores)


def tables():
    import numpy as np
    f = np.float32
    k, q = np.arange(P)[None, :], np.arange(P)[:, None]
    cut = lambda keep: np.where(keep, 0, MASKED).astype(f)
    j = np.arange(192)[None, :]
    masks = np.concatenate([cut((k <= q) & (q - k <= 64)), cut((q <= j) & (j <= q + 64)), cut(k <= q)], 1)
    p = np.arange(P)
    signs = np.zeros((P, 8), f)
    signs[:, 0] = -((p % 64) >= 32).astype(f)
    signs[:, 1] = -((p // 16) % 2).astype(f)
    signs[:, 2] = -((p % 32) >= 16).astype(f)
    signs[:, 3] = -((p // 8) % 2).astype(f)
    signs[:, 4] = -(p >= 64).astype(f)
    half = 64
    inv = (f(1.0) / np.power(f(10000.0), np.arange(half, dtype=f) / f(half))).astype(f)
    fr = (np.arange(SEQ, dtype=f)[None, :] * inv[:, None]).astype(f)
    cos, sin = np.cos(fr).astype(f), np.sin(fr).astype(f)
    rope0 = np.stack([np.concatenate([cos, cos]), np.concatenate([sin, -sin])], 1)

    def latent(length, dim):
        inv = (f(1.0) / np.power(f(10000.0), np.arange(0, dim, 2, dtype=f) / f(dim))).astype(f)
        fr = (np.arange(length, dtype=f)[:, None] * inv[None, :]).astype(f)
        return np.repeat(np.sin(fr).astype(f), 2, -1), np.repeat(np.cos(fr).astype(f), 2, -1)

    sq, cq = latent(SEQ, 192)
    ropeq = np.stack([cq[:, :96].T, cq[:, 96:].T, -sq[:, :96].T, sq[:, 96:].T], 1)
    sk, ck = latent(CTX, LAT)
    sk = np.concatenate([-sk[:, :32], sk[:, 32:]], 1)
    pad = np.zeros((KT * P - CTX, LAT), f)
    ropek = np.stack([np.concatenate([a, pad]).reshape(KT, P, LAT).transpose(1, 0, 2) for a in (ck, sk)], 1)
    d = np.arange(D).reshape(2, 1, P)
    e16 = (np.arange(16)[None, :, None] == d // 16).astype(f).transpose(1, 0, 2)
    e8 = (np.arange(32)[None, :, None] == d // 8).astype(f).transpose(1, 0, 2)
    return {"ident": np.eye(P, dtype=f), "masks": masks, "signs": signs, "rope0": rope0,
            "ropeq": ropeq, "ropek": ropek, "expand16": e16, "expand8": e8,
            "iota8": np.tile(np.arange(8, dtype=f), (P, 1))}


def layouts(i):
    import numpy as np

    def rows(w):
        return w.reshape(w.shape[0] // P, P, w.shape[1]).transpose(1, 0, 2)

    def repeat_heads(w, hd, per_tile, shared=1):
        h = w.reshape(w.shape[0], -1, 1, hd)
        h = np.repeat(h, shared, axis=1)
        return np.broadcast_to(h, (w.shape[0], h.shape[1], 4, hd)).reshape(w.shape[0], -1)

    a = {}
    x = i["x"].reshape(BATCH * SEQ, D)
    a["x"], a["xT"] = x, x.T
    ctx = i["ctx_512"]
    pad = np.zeros((BATCH, KT * P - CTX, LAT), ctx.dtype)
    a["ctx"] = np.concatenate([ctx, pad], 1).reshape(BATCH, KT, P, LAT).transpose(0, 2, 1, 3)
    ct = ctx[:, :SEQ].transpose(2, 0, 1).reshape(LAT, BATCH * SEQ)
    a["ctxT"] = np.concatenate([ct, ct])
    a["a_wkv"] = rows(np.concatenate([i["L0_attn_wk"].T, i["L0_attn_wv"].T], 1)).reshape(P, -1)
    wq = rows(i["L0_attn_wq"].T).reshape(P, DC, 2, 2, 512)
    a["a_wq"] = wq.transpose(2, 0, 3, 1, 4).reshape(2, P, 2048)
    wo = i["L0_attn_wo"].T.reshape(2, 8, P, D)
    a["a_wo"] = wo.transpose(0, 2, 1, 3).reshape(2, P, 2048)
    wk, wv = i["L0_xattn_Wkv_expand"][:D].T, i["L0_xattn_Wkv_expand"][D:].T
    a["b_wq"] = rows(repeat_heads(i["L0_xattn_Wq"].T, 16, 2))
    a["b_wk"] = np.concatenate([repeat_heads(wk, 16, 2)] * 2)[:, None, :]
    a["b_wv"] = np.concatenate([wv] * 2)[:, None, :]
    a["b_wo"] = rows(i["L0_xattn_Wout"].T)
    a["d_wq"] = rows(repeat_heads(i["L1_attn_Wq"], 8, 4))
    a["d_wk"] = rows(repeat_heads(i["L1_attn_Wk"], 8, 4, shared=4))
    a["d_wv"] = rows(i["L1_attn_Wv"])
    a["d_wo"] = rows(i["L1_attn_Wo"])
    a["f_wq"] = rows(repeat_heads(i["L1_ffn_Wq"].T, 16, 2))
    a["f_wk"] = rows(repeat_heads(i["L1_ffn_Wk"].T, 16, 2))
    a["f_wv"] = rows(i["L1_ffn_Wv"].T)
    a["f_wo"] = rows(i["L1_ffn_Wo"].T)
    a["f_ln"] = np.concatenate([rows(i["L1_ffn_w_ln1"][:, None])[:, :, 0], rows(i["L1_ffn_w_ln2"][:, None])[:, :, 0]], 1)
    def experts(w1, w3, w2):
        pack = lambda w, n: w.reshape(8, n, P, -1).transpose(0, 2, 1, 3).reshape(8, P, -1)
        return np.concatenate([pack(w1, DC), pack(w3, DC), pack(w2, 4)], 2)
    a["c_w"] = experts(i["L0_ffn_w1"], i["L0_ffn_w3"], i["L0_ffn_w2"])
    a["c_gate"] = rows(i["L0_ffn_w_gate"])
    a["g_w"] = experts(i["L1_ffn_Wg"].transpose(0, 2, 1), i["L1_ffn_Wu"].transpose(0, 2, 1),
                       i["L1_ffn_Wd"].transpose(0, 2, 1))
    a["g_gate"] = rows(i["L1_ffn_Wr"].T)
    wq = i["L1_xattn_Wq"].reshape(16, P, D)
    wo = i["L1_xattn_Wo"].T.reshape(16, P, D)
    kv = i["L1_xattn_w_kc_kv"]
    a["e_w"] = np.concatenate([wq, i["L1_xattn_w_kc_q"], wo, kv, kv], 2)
    kr = i["L1_xattn_W_kr"].transpose(0, 2, 1)
    a["e_wr"] = np.concatenate([i["L1_xattn_W_qr"].transpose(0, 2, 1), kr, kr], 2)
    return {k: np.ascontiguousarray(v) for k, v in a.items()}


def kernel(**inputs):
    import numpy as np
    import concourse.bacc as bacc
    from concourse.bass_utils import run_bass_kernel_spmd

    nc = bacc.Bacc("TRN2", target_bir_lowering=False, num_devices=1)
    arrays = {**layouts({k: np.asarray(v) for k, v in inputs.items()}), **tables()}
    t = {k: nc.dram_tensor("in_" + k, v.shape, mybir.dt.from_np(v.dtype), kind="ExternalInput").ap()
         for k, v in arrays.items()}
    out = nc.dram_tensor("out", (BATCH * SEQ, D), F32, kind="ExternalOutput").ap()
    decoder(nc, t, out)
    r = run_bass_kernel_spmd(nc, [{"in_" + k: v for k, v in arrays.items()}], core_ids=[0])
    return r.results[0]["out"].reshape(BATCH, SEQ, D)
```
